# Optimizing a Trainium2 kernel written in Bass

```python
import numpy as np
import jax
import jax.numpy as jnp

def _softmax(x, axis=-1):
    return jax.nn.softmax(x, axis=axis)

def _gelu(x):
    return jax.nn.gelu(x, approximate=True)

def _silu(x):
    return jax.nn.silu(x)

def _sigmoid(x):
    return jax.nn.sigmoid(x)

def _layernorm(x, axis=-1, eps=1e-05):
    m = jnp.mean(x, axis=axis, keepdims=True)
    v = jnp.var(x, axis=axis, keepdims=True)
    return (x - m) / jnp.sqrt(v + eps)

def _scatter_add(tgt, idx, src, axis=0):
    return tgt.at[idx].add(src)

def _segment_sum(src, seg, n):
    return jax.ops.segment_sum(src, seg, n)
kernel_name = 'mk_early_fusion_embed_d1_tok_img256_r4_a2ace6'

def setup_inputs(seed: int=0):
    np.random.seed(seed)
    _w = jnp.asarray

    def _rec_inputs():
        import jax
        import jax.numpy as jnp
        _rk = jax.random.key(seed)
        x = -7.10856e-05 + 0.999911 * jax.random.normal(jax.random.fold_in(_rk, 1), (8, 64, 64, 64), jnp.float32)
        x_txt = jax.random.randint(jax.random.fold_in(_rk, 51), (8, 128), 0, 99998, jnp.int32)
        return (x, x_txt)
    x, x_txt = _rec_inputs()

    def _L0_tok_setup():
        import jax, jax.numpy as jnp
        import numpy as np
        GS = 8
        NH = 8
        DM = 64
        B, W, H = (4, 64, 64)
        key = jax.random.key(seed)
        ks = jax.random.split(key, 5)
        s = 0.02
        return {'x': jax.random.normal(ks[0], (B, DM, W, H), dtype=jnp.float32), 'Wq': jax.random.normal(ks[1], (DM, DM), dtype=jnp.float32) * s, 'bq': jnp.zeros((DM,), dtype=jnp.float32), 'Wk': jax.random.normal(ks[2], (DM, DM), dtype=jnp.float32) * s, 'bk': jnp.zeros((DM,), dtype=jnp.float32), 'Wv': jax.random.normal(ks[3], (DM, DM), dtype=jnp.float32) * s, 'bv': jnp.zeros((DM,), dtype=jnp.float32), 'Wo': jax.random.normal(ks[4], (DM, DM), dtype=jnp.float32) * s, 'bo': jnp.zeros((DM,), dtype=jnp.float32)}
    _L0_tok_all = _L0_tok_setup()
    _L0_tok_in = {k: v for k, v in _L0_tok_all.items() if k in ('Wq', 'bq', 'Wk', 'bk', 'Wv', 'bv', 'Wo', 'bo')}
    del _L0_tok_all

    def _L0_txt_setup():
        import jax, jax.numpy as jnp
        import numpy as np
        P = 100003
        M = 12500
        IC = 4
        NUM_SPECIAL = 4
        A_VALS = np.array([12345, 20011], dtype=np.int32)
        B_VALS = np.array([6789, 54321], dtype=np.int32)
        VOCAB = 25000
        EMBED = 64
        NUM_HASHES = 2
        B, S = (64, 512)
        key = jax.random.key(seed)
        k1, k2, k3 = jax.random.split(key, 3)
        x = jax.random.randint(k1, (B, S), 0, VOCAB, dtype=jnp.int32)
        shared = 0.02 * jax.random.normal(k2, (M + IC, EMBED), dtype=jnp.float32)
        shared = shared.at[0].set(0.0)
        hw = jax.random.normal(k3, (VOCAB, NUM_HASHES), dtype=jnp.float32)
        hw = hw.at[0].set(0.0)
        return {'x': x, 'shared_embedding': shared, 'hash_weights_table': hw}
    _L0_txt_all = _L0_txt_setup()
    _L0_txt_in = {k: v for k, v in _L0_txt_all.items() if k in ('shared_embedding', 'hash_weights_table')}
    del _L0_txt_all

    def _L0_attn_setup():
        import jax, jax.numpy as jnp
        import numpy as np
        B, T, F, H = (128, 256, 64, 128)

        def _lstm(xWb, U, reverse=False, return_sequences=False):
            Hn = U.shape[0]
            xs = jnp.swapaxes(xWb, 0, 1)
            h0 = jnp.zeros((xWb.shape[0], Hn), xWb.dtype)
            c0 = h0

            def step(carry, xw):
                h, c = carry
                z = xw + h @ U
                i, f, g, o = jnp.split(z, 4, axis=-1)
                i = jax.nn.sigmoid(i)
                f = jax.nn.sigmoid(f)
                g = jnp.tanh(g)
                o = jax.nn.sigmoid(o)
                c = f * c + i * g
                h = o * jnp.tanh(c)
                return ((h, c), h)
            (hT, _), hs = jax.lax.scan(step, (h0, c0), xs, reverse=reverse)
            if return_sequences:
                return jnp.swapaxes(hs, 0, 1)
            return hT
        key = jax.random.key(seed)
        ks = jax.random.split(key, 9)
        g = lambda k, shape: jax.random.normal(k, shape, jnp.float32) * 0.05
        return {'x': jax.random.uniform(ks[0], (B, T, F), jnp.float32), 'Wf': g(ks[1], (F, 4 * H)), 'Uf': g(ks[2], (H, 4 * H)), 'bf': jnp.zeros((4 * H,), jnp.float32), 'Wb': g(ks[3], (F, 4 * H)), 'Ub': g(ks[4], (H, 4 * H)), 'bb': jnp.zeros((4 * H,), jnp.float32), 'Wd': g(ks[5], (2 * H, 4 * H)), 'Ud': g(ks[6], (H, 4 * H)), 'bd': jnp.zeros((4 * H,), jnp.float32), 'Wo': g(ks[7], (H, F)), 'bo': jnp.zeros((F,), jnp.float32)}
    _L0_attn_all = _L0_attn_setup()
    _L0_attn_in = {k: v for k, v in _L0_attn_all.items() if k in ('Wf', 'Uf', 'bf', 'Wb', 'Ub', 'bb', 'Wd', 'Ud', 'bd', 'Wo', 'bo')}
    del _L0_attn_all

    def _L0_ffn_setup():
        import jax, jax.numpy as jnp
        import numpy as np
        B, S, D = (8, 1024, 64)
        H = 4 * D
        CAPACITY = 0.5
        key = jax.random.key(seed)
        ks = jax.random.split(key, 6)
        x = jax.random.normal(ks[0], (B, S, D), dtype=jnp.float32)
        attention_mask = jnp.zeros((B, 1, 1, S), dtype=jnp.float32)
        wr = jax.random.normal(ks[1], (D, 1), dtype=jnp.float32) * 0.02
        br = jnp.zeros((1,), dtype=jnp.float32)
        w1 = jax.random.normal(ks[2], (D, H), dtype=jnp.float32) * 0.02
        b1 = jnp.zeros((H,), dtype=jnp.float32)
        w2 = jax.random.normal(ks[3], (H, D), dtype=jnp.float32) * 0.02
        b2 = jnp.zeros((D,), dtype=jnp.float32)
        return {'x': x, 'attention_mask': attention_mask, 'wr': wr, 'br': br, 'w1': w1, 'b1': b1, 'w2': w2, 'b2': b2}
    _L0_ffn_all = _L0_ffn_setup()
    _L0_ffn_in = {k: v for k, v in _L0_ffn_all.items() if k in ('attention_mask', 'wr', 'br', 'w1', 'b1', 'w2', 'b2')}
    del _L0_ffn_all
    return {'x': x, 'x_txt': x_txt, 'L0_tok_Wq': _L0_tok_in['Wq'], 'L0_tok_bq': _L0_tok_in['bq'], 'L0_tok_Wk': _L0_tok_in['Wk'], 'L0_tok_bk': _L0_tok_in['bk'], 'L0_tok_Wv': _L0_tok_in['Wv'], 'L0_tok_bv': _L0_tok_in['bv'], 'L0_tok_Wo': _L0_tok_in['Wo'], 'L0_tok_bo': _L0_tok_in['bo'], 'L0_txt_shared_embedding': _L0_txt_in['shared_embedding'], 'L0_txt_hash_weights_table': _L0_txt_in['hash_weights_table'], 'L0_attn_Wf': _L0_attn_in['Wf'], 'L0_attn_Uf': _L0_attn_in['Uf'], 'L0_attn_bf': _L0_attn_in['bf'], 'L0_attn_Wb': _L0_attn_in['Wb'], 'L0_attn_Ub': _L0_attn_in['Ub'], 'L0_attn_bb': _L0_attn_in['bb'], 'L0_attn_Wd': _L0_attn_in['Wd'], 'L0_attn_Ud': _L0_attn_in['Ud'], 'L0_attn_bd': _L0_attn_in['bd'], 'L0_attn_Wo': _L0_attn_in['Wo'], 'L0_attn_bo': _L0_attn_in['bo'], 'L0_ffn_attention_mask': _L0_ffn_in['attention_mask'], 'L0_ffn_wr': _L0_ffn_in['wr'], 'L0_ffn_br': _L0_ffn_in['br'], 'L0_ffn_w1': _L0_ffn_in['w1'], 'L0_ffn_b1': _L0_ffn_in['b1'], 'L0_ffn_w2': _L0_ffn_in['w2'], 'L0_ffn_b2': _L0_ffn_in['b2']}

def reference(x, x_txt, L0_tok_Wq, L0_tok_bq, L0_tok_Wk, L0_tok_bk, L0_tok_Wv, L0_tok_bv, L0_tok_Wo, L0_tok_bo, L0_txt_shared_embedding, L0_txt_hash_weights_table, L0_attn_Wf, L0_attn_Uf, L0_attn_bf, L0_attn_Wb, L0_attn_Ub, L0_attn_bb, L0_attn_Wd, L0_attn_Ud, L0_attn_bd, L0_attn_Wo, L0_attn_bo, L0_ffn_attention_mask, L0_ffn_wr, L0_ffn_br, L0_ffn_w1, L0_ffn_b1, L0_ffn_w2, L0_ffn_b2):
    import jax
    import jax.numpy as jnp

    def _L0_tok_ref(x, Wq, bq, Wk, bk, Wv, bv, Wo, bo):
        import jax, jax.numpy as jnp
        import numpy as np
        GS = 8
        NH = 8
        DM = 64
        B, W, H = (4, 64, 64)
        b, d, w, h = x.shape
        gw, gh = (w // GS, h // GS)
        n = gw * gh
        L = GS * GS
        dh = d // NH
        q = x.reshape(b, d, gw, GS, gh, GS).mean(axis=(3, 5))
        q = q.reshape(b, d, n).transpose(0, 2, 1).reshape(b * n, 1, d)
        kv = x.transpose(0, 2, 3, 1)
        kv = kv.reshape(b, gw, GS, gh, GS, d)
        kv = kv.transpose(0, 1, 3, 2, 4, 5).reshape(b * n, L, d)
        qp = (q @ Wq.T + bq).reshape(b * n, 1, NH, dh).transpose(0, 2, 1, 3)
        kp = (kv @ Wk.T + bk).reshape(b * n, L, NH, dh).transpose(0, 2, 1, 3)
        vp = (kv @ Wv.T + bv).reshape(b * n, L, NH, dh).transpose(0, 2, 1, 3)
        scores = jnp.einsum('bhqd,bhkd->bhqk', qp, kp) / jnp.sqrt(jnp.float32(dh))
        attn = jax.nn.softmax(scores, axis=-1)
        ctx = jnp.einsum('bhqk,bhkd->bhqd', attn, vp)
        ctx = ctx.transpose(0, 2, 1, 3).reshape(b * n, 1, d)
        attn_out = ctx @ Wo.T + bo
        out = q + attn_out
        return out.reshape(b, n, d)

    def _L0_txt_ref(x, shared_embedding, hash_weights_table):
        import jax, jax.numpy as jnp
        import numpy as np
        P = 100003
        M = 12500
        IC = 4
        NUM_SPECIAL = 4
        A_VALS = np.array([12345, 20011], dtype=np.int32)
        B_VALS = np.array([6789, 54321], dtype=np.int32)
        VOCAB = 25000
        EMBED = 64
        NUM_HASHES = 2
        B, S = (64, 512)
        hw = hash_weights_table[x]
        a = jnp.asarray(A_VALS)
        b = jnp.asarray(B_VALS)
        hashes = (a * x[..., None] + b) % P % M + IC
        hashes = jnp.where(x[..., None] < NUM_SPECIAL, x[..., None], hashes)
        embs = shared_embedding[hashes]
        return jnp.einsum('bsh,bshe->bse', hw, embs)

    def _L0_attn_ref(x, Wf, Uf, bf, Wb, Ub, bb, Wd, Ud, bd, Wo, bo):
        import jax, jax.numpy as jnp
        import numpy as np
        B, T, F, H = (128, 256, 64, 128)

        def _lstm(xWb, U, reverse=False, return_sequences=False):
            Hn = U.shape[0]
            xs = jnp.swapaxes(xWb, 0, 1)
            h0 = jnp.zeros((xWb.shape[0], Hn), xWb.dtype)
            c0 = h0

            def step(carry, xw):
                h, c = carry
                z = xw + h @ U
                i, f, g, o = jnp.split(z, 4, axis=-1)
                i = jax.nn.sigmoid(i)
                f = jax.nn.sigmoid(f)
                g = jnp.tanh(g)
                o = jax.nn.sigmoid(o)
                c = f * c + i * g
                h = o * jnp.tanh(c)
                return ((h, c), h)
            (hT, _), hs = jax.lax.scan(step, (h0, c0), xs, reverse=reverse)
            if return_sequences:
                return jnp.swapaxes(hs, 0, 1)
            return hT
        h_fwd = _lstm(x @ Wf + bf, Uf, reverse=False)
        h_bwd = _lstm(x @ Wb + bb, Ub, reverse=True)
        latent = jnp.concatenate([h_fwd, h_bwd], axis=-1)
        rep = jnp.broadcast_to(latent[:, None, :], (x.shape[0], x.shape[1], 2 * H))
        dec = _lstm(rep @ Wd + bd, Ud, return_sequences=True)
        return dec @ Wo + bo

    def _L0_ffn_ref(x, attention_mask, wr, br, w1, b1, w2, b2):
        import jax, jax.numpy as jnp
        import numpy as np
        B, S, D = (8, 1024, 64)
        H = 4 * D
        CAPACITY = 0.5
        b, s, d = x.shape
        weights = (jnp.einsum('bsd,do->bso', x, wr) + br)[..., 0]
        k = max(1, int(CAPACITY * s))
        kk = k - 1 if k > 1 else 1
        _, idx = jax.lax.top_k(weights, k)
        sel_idx = idx[:, :kk]
        sel = jnp.take_along_axis(x, sel_idx[:, :, None], axis=1)
        h = jax.nn.gelu(jnp.einsum('bkd,dh->bkh', sel, w1) + b1)
        y = jnp.einsum('bkh,hd->bkd', h, w2) + b2
        w_sel = jnp.take_along_axis(weights, sel_idx, axis=1)
        y = y * w_sel[..., None]
        batch_idx = jnp.arange(b)[:, None]
        processed = jnp.zeros_like(x).at[batch_idx, sel_idx].set(y)
        return processed + x
    h = _L0_tok_ref(x, L0_tok_Wq, L0_tok_bq, L0_tok_Wk, L0_tok_bk, L0_tok_Wv, L0_tok_bv, L0_tok_Wo, L0_tok_bo)
    h = jnp.concatenate([h, _L0_txt_ref(x_txt, L0_txt_shared_embedding, L0_txt_hash_weights_table)], axis=1)
    h = h + _L0_attn_ref(_layernorm(h, axis=-1), L0_attn_Wf, L0_attn_Uf, L0_attn_bf, L0_attn_Wb, L0_attn_Ub, L0_attn_bb, L0_attn_Wd, L0_attn_Ud, L0_attn_bd, L0_attn_Wo, L0_attn_bo)
    h = h + _L0_ffn_ref(_layernorm(h, axis=-1), L0_ffn_attention_mask, L0_ffn_wr, L0_ffn_br, L0_ffn_w1, L0_ffn_b1, L0_ffn_w2, L0_ffn_b2)
    return h

_drawn_inputs = setup_inputs


def setup_inputs(seed=0):
    import zlib

    import numpy as np

    out = dict(_drawn_inputs(seed))
    spreads = {'L0_tok_bq': (0.0, 0.8),
     'L0_tok_bk': (0.0, 0.8),
     'L0_tok_bv': (0.0, 0.1),
     'L0_tok_bo': (0.0, 0.1),
     'L0_attn_bf': (0.0, 0.1),
     'L0_attn_bb': (0.0, 0.1),
     'L0_attn_bd': (0.0, 0.1),
     'L0_attn_bo': (0.0, 0.1),
     'L0_ffn_b1': (0.0, 0.8),
     'L0_ffn_b2': (0.0, 0.8)}
    factors = {'L0_tok_Wq': 8.0,
     'L0_tok_Wk': 8.0,
     'L0_tok_Wv': 5.769,
     'L0_ffn_wr': 8.0,
     'L0_ffn_w1': 8.0,
     'L0_ffn_w2': 8.0}
    for name, (base, spread) in spreads.items():
        noise = np.random.default_rng([zlib.crc32(name.encode()), seed]).standard_normal(out[name].shape)
        drawn = base * np.exp(spread * noise) if base else spread * noise
        out[name] = jnp.asarray(drawn.astype(out[name].dtype))
    for name, factor in factors.items():
        out[name] = (out[name] * factor).astype(out[name].dtype)
    return out
```

```python
from contextlib import ExitStack

import concourse.bass as bass
from concourse import mybir

F32 = mybir.dt.float32
F16 = mybir.dt.float16
BF16 = mybir.dt.bfloat16
I32 = mybir.dt.int32
ALU = mybir.AluOpType
ACT = mybir.ActivationFunctionType
AX = mybir.AxisListType

B, D, W = 8, 64, 64
GS, NH = 8, 8
T_IMG, T_TXT = (W // GS) ** 2, 128
T = T_IMG + T_TXT
HID = 128
PAIRS = B // 2
STRIPS = W // GS
SC = GS * B
TOK = T * B
CH_T = 16
CC = CH_T * B
CHUNKS = T // CH_T
TXT_CHUNKS = T_TXT // CH_T
HALF = T // 2
KEEP = max(1, int(0.5 * T)) - 1
EPS = 1e-5

HASH_P, HASH_M, HASH_IC = 100003, 12500, 4
HASH_A = (12345, 20011)
HASH_B = (6789, 54321)
VOCAB = 25000
DIGIT = 128

H_SCALE = 2.0 ** 15
U_SCALE = 2.0 ** 4
SEED_SCALE = 2.0 ** 5
SEED_IDENT = H_SCALE * U_SCALE / SEED_SCALE
Z_ACT = 0.5 / (H_SCALE * U_SCALE)
NEG = -30000.0
GELU_C, GELU_S = 0.044715, 0.7978845608028654

PA = {}
_at = 0
for _name, _n in (("ident", 128), ("wq", 128), ("wk", 128), ("wv", 128), ("wo0", D), ("wo1", D), ("res0", D), ("res1", D),
                  ("headmask", 16), ("groupmask", 512), ("bq", 1), ("bv", 1),
                  ("Uf", 512), ("Ub", 512), ("Ud", 512), ("Wd0", 512), ("Wd1", 512), ("bd", 4),
                  ("Wo", D), ("w2a", 128), ("w2b", 128), ("b2", 1), ("before", HALF)):
    PA[_name] = (_at, _at + _n)
    _at += _n
PA_N = _at
PB = {}
_at = 0
for _name, _n in (("center", 128), ("mean", 128), ("bo", 1), ("boA", 1),
                  ("Wf", 512), ("Wb", 512), ("w1", 256), ("wr", 128)):
    PB[_name] = (_at, _at + _n)
    _at += _n
PB_N = _at


def build(nc, x, ids, table, hashw, packa, packb, out):
    with ExitStack() as ctx:
        def sb(name, shape, dt=F32):
            return ctx.enter_context(nc.sbuf_tensor(name, shape, dt))

        def psum(name):
            return ctx.enter_context(nc.psum_tensor(name, [128, 512], F32))

        def sem(name):
            return ctx.enter_context(nc.semaphore(name))

        ca = sb("ca", [128, PA_N])
        cb = sb("cb", [65, PB_N])

        def A(name, rows=128):
            return ca[0:rows, PA[name][0]:PA[name][1]]

        def Bc(name, rows=D):
            return cb[0:rows, PB[name][0]:PB[name][1]]

        X = sb("X", [128, 2, PAIRS * GS * W])
        Xv = [X[:, s, :].rearrange("q (p w h) -> q p w h", p=PAIRS, w=GS) for s in range(2)]
        Xr = sb("Xr", [128, 2, PAIRS, 4, 128])
        qsum = sb("qsum", [128, PAIRS * GS])
        qp = sb("qp", [128, PAIRS * GS])
        qm = sb("qm", [128, PAIRS * GS * 16])
        qk = sb("qk", [128, PAIRS * GS * 16])
        score = sb("score", [128, 512])
        negmax = sb("negmax", [128, 4])
        esum = sb("esum", [128, 4])
        rsum = sb("rsum", [128, 4])
        prob = sb("prob", [128, 512])
        xT = sb("xT", [128, PAIRS * 4 * 128])
        probT = sb("probT", [128, 512])
        ysb = sb("ysb", [128, 512])
        cmask = sb("cmask", [128, 512])
        ctxv = sb("ctxv", [128, PAIRS * GS])
        ctxb = sb("ctxb", [128, PAIRS * GS])
        h1T = sb("h1T", [D, TOK])

        idx_i = sb("idx_i", [128, B], I32)
        idf = sb("idf", [128, B])
        hp = sb("hp", [128, 2 * B])
        hx = sb("hx", [128, 2 * B])
        hq = sb("hq", [128, 2 * B], I32)
        hm = sb("hm", [128, 2 * B])
        small = sb("small", [128, B])
        hidx = sb("hidx", [128, 2 * B], I32)
        widx = sb("widx", [128, B], I32)
        emb = sb("emb", [128, 2, B, D])
        hwt = sb("hwt", [128, B, 2])
        txt = sb("txt", [128, B, D])

        sq = sb("sq", [D, CC])
        varp = sb("varp", [D, CC])
        neg_half = sb("neg_half", [D, CC])
        rstd = sb("rstd", [D, CC])
        xn = sb("xn", [65, CC])
        XW = [sb(f"XW{p}", [128, 2 * T * 32], F16) for p in range(2)]

        ident16 = sb("ident16", [128, 128], F16)
        Ua = sb("Ua", [128, 3 * 512], F16)
        Ul = sb("Ul", [128, 3 * 512], F16)
        G = sb("G", [128, 2, 5, 16])
        prod = sb("prod", [128, 2, 16])
        osc = sb("osc", [128, 16])
        tc = sb("tc", [128, 16])
        H = sb("H", [128, 16])
        ha = sb("ha", [128, 16], F16)
        hb = sb("hb", [128, 16], F16)
        zc = sb("zc", [128, 32])
        zcs = [sb(f"zcs{p}", [128, 32], F16) for p in range(2)]
        hist = sb("hist", [128, TOK])

        h2 = sb("h2", [D, CC])
        wrow = sb("wrow", [128, TOK])
        usq = sb("usq", [128, 256])
        uin = sb("uin", [128, 256])
        uin2 = sb("uin2", [128, 256])
        uth = sb("uth", [128, 256])
        ug = sb("ug", [128, 256])
        parts = sb("parts", [128, CC])
        ab = sb("ab", [128, CHUNKS * 128])
        wcol = sb("wcol", [HALF, 2 * B])
        beats = [[sb(f"beats{j}{i}", [HALF, HALF * B], BF16) for i in range(2)] for j in range(2)]
        equal = [sb(f"equal{j}", [HALF, HALF * B], BF16) for j in range(2)]
        tie = [sb(f"tie{j}", [HALF, HALF * B], BF16) for j in range(2)]
        ones16 = sb("ones16", [HALF, 2], BF16)
        keep = sb("keep", [128, CHUNKS])
        routed = sb("routed", [128, CHUNKS, D])
        fin = sb("fin", [128, CHUNKS, D])

        zA, zB, p_small, p_a, p_b, p_x0, p_x1, p_t = [psum(n) for n in (
            "zA", "zB", "p_small", "p_a", "p_b", "p_x0", "p_x1", "p_t")]
        p_x = [p_x0, p_x1]

        s_ca, s_cb, s_ids = sem("s_ca"), sem("s_cb"), sem("s_ids")
        s_x = [sem("s_x0"), sem("s_x1")]
        xt_copied = [sem("xt_copied0"), sem("xt_copied1")]
        S = {n: sem("s_" + n) for n in (
            "xr qsum qp_mm qp qm qk_mm qk score_mm score negmax exp rsum prob xt_mm pt_mm pt y_mm y c_mm cmask ctxv ctxb "
            "o_mm h1 cen sq var varp rstd xn proj seed_a seed_b hash hidx gath txt tt_mm tt_copy weights memset "
            "zgfi zo gates ogate prod cell osc tanhc ha hfull hb hist lat zc zcs "
            "f_mm h2 r_mm wrow u_mm usq uin uin2 uth ug y2_mm bt at ab_mm ab wc_mm wcol equal beats rank keep routed fin out"
        ).split()}

        block = ctx.enter_context(nc.Block())
        x_dram = x.rearrange("(p two) c (g w) h -> g (two c) p (w h)", two=2, w=GS)

        LN_TXT = STRIPS
        LN_OUT = STRIPS + TXT_CHUNKS
        WEIGHTS = 19

        @block.sync
        def _(sp):
            def load_strip(n, s):
                sp.dma_start(X[:, s, :].rearrange("q (p n) -> q p n", p=PAIRS),
                             x_dram[bass.ds(n, 1)].rearrange("g q p n -> (g q) p n")).then_inc(s_x[s], 16)
            sp.dma_start(idx_i[:, :], ids).then_inc(s_ids, 16)
            load_strip(0, 0)
            sp.dma_start(ca[:, :], packa).then_inc(s_ca, 16)
            sp.dma_start(cb[:, :], packb).then_inc(s_cb, 16)
            load_strip(1, 1)
            with sp.Fori(1, STRIPS // 2) as i:
                for s in range(2):
                    sp.wait_ge(S["qsum"], 2 * i + s - 1)
                    sp.wait_ge(S["xr"], 2 * i + s - 1)
                    load_strip(2 * i + s, s)
            for c in range(4):
                sp.wait_ge(S["fin"], c + 1)
                k0, k1 = 3 * c, 3 * c + 3
                sp.dma_start(out[k0 * CC:k1 * CC, :].rearrange("(k p) d -> p k d", p=128),
                             fin[:, k0:k1, :]).then_inc(S["out"], 16)
            sp.wait_ge(S["out"], 64)

        @block.gpsimd
        def _(pool):
            pool.memset(G[:, :, :, :], 0.0).then_inc(S["memset"], 1)
            pool.memset(neg_half[:, :], -0.5).then_inc(S["memset"], 1)
            pool.memset(ones16[:, :], 1.0).then_inc(S["memset"], 1)
            pool.wait_ge(S["memset"], 3)
            pool.memset(xn[64:65, :], 1.0).then_inc(S["memset"], 1)
            pool.wait_ge(S["memset"], 4)
            pool.wait_ge(S["hidx"], 2)
            for b in range(B):
                for k in range(2):
                    pool.indirect_dma_start(
                        out=emb[:, k, b, :], out_offset=None, in_=table,
                        in_offset=bass.IndirectOffsetOnAxis(ap=hidx[:, k * B + b:k * B + b + 1], axis=0)
                    ).then_inc(S["gath"], 16)
                pool.indirect_dma_start(
                    out=hwt[:, b, :], out_offset=None, in_=hashw,
                    in_offset=bass.IndirectOffsetOnAxis(ap=widx[:, b:b + 1], axis=0)
                ).then_inc(S["gath"], 16)

            def power(q, n):
                pool.wait_ge(S["varp"], q + 1)
                pool.tensor_tensor(rstd[:, 0:n], varp[:, 0:n], neg_half[:, 0:n], ALU.pow).then_inc(S["rstd"], 1)

            def regroup(s):
                for p in range(PAIRS):
                    last = pool.tensor_copy(Xr[:, s, p, :, :].rearrange("q j (w c) -> q j w c", c=16),
                                            Xv[s][:, p, :, :].rearrange("q w (j c) -> q j w c", c=16))
                last.then_inc(S["xr"], 1)

            for s in range(2):
                pool.wait_ge(s_x[s], 16)
                regroup(s)
            with pool.Fori(0, STRIPS // 2 - 1) as i:
                for s in range(2):
                    pool.wait_ge(s_x[s], 16 * (i + 2))
                    power(2 * i + s, SC)
                    regroup(s)
            for s in range(2):
                power(STRIPS - 2 + s, SC)
            with pool.Fori(0, TXT_CHUNKS) as i:
                power(i + LN_TXT, CC)
            with pool.Fori(0, CHUNKS) as i:
                power(i + LN_OUT, CC)

        @block.tensor
        def _(pe):
            def mm(o, l, r, start=True, stop=True):
                return pe.matmul(o, l, r, start=start, stop=stop, skip_group_check=True)

            def normalise(q, src, n):
                mm(p_small[:, 0:n], Bc("center"), src).then_inc(S["cen"], 1)
                pe.wait_ge(S["sq"], q + 1)
                mm(p_small[:, 128:128 + n], Bc("mean"), sq[:, 0:n]).then_inc(S["var"], 1)

            def project(q, n):
                pe.wait_ge(S["xn"], q + 1)
                for d, name in enumerate(("Wf", "Wb")):
                    for g in range(4):
                        last = mm(p_x[d][:, g * n:g * n + n], Bc(name, 65)[:, g * 128:g * 128 + 128], xn[0:65, 0:n])
                    last.then_inc(S["proj"], 1)

            def strip(i, s, first):
                n = 2 * i + s
                later = not first or s > 0
                pe.wait_ge(S["xr"], n + 1)
                if later:
                    pe.wait_ge(S["seed_b"], 2 * n)
                for r in range(PAIRS):
                    if later or r >= 2:
                        pe.wait_ge(xt_copied[r % 2], 2 * n + r // 2)
                    for j in range(4):
                        last = pe.transpose(p_x[r % 2][:, j * 128:j * 128 + 128], Xr[:, s, r, j, :], A("ident"))
                    last.then_inc(S["xt_mm"], 1)
                pe.wait_ge(S["qsum"], n + 1)
                mm(p_small[:, 0:32], A("wq"), qsum[:, :]).then_inc(S["qp_mm"], 1)
                pe.wait_ge(S["qm"], n + 1)
                mm(p_a[:, :], A("wk"), qm[:, :]).then_inc(S["qk_mm"], 1)
                pe.wait_ge(S["qk"], n + 1)
                for p in range(PAIRS):
                    for j in range(4):
                        c = (p * GS + 2 * j) * 16
                        last = mm(p_b[32 * p:32 * p + 32, j * 128:j * 128 + 128], qk[:, c:c + 32], Xr[:, s, p, j, :])
                last.then_inc(S["score_mm"], 1)
                pe.wait_ge(S["prob"], n + 1)
                for j in range(4):
                    last = pe.transpose(p_b[:, j * 128:j * 128 + 128], prob[:, j * 128:j * 128 + 128], A("ident"))
                last.then_inc(S["pt_mm"], 1)
                pe.wait_ge(xt_copied[0], 2 * n + 2)
                pe.wait_ge(xt_copied[1], 2 * n + 2)
                pe.wait_ge(S["pt"], n + 1)
                for p in range(PAIRS):
                    for j in range(4):
                        c = (p * 4 + j) * 128
                        last = mm(p_a[:, (p * 4 + j) * 32:(p * 4 + j) * 32 + 32], xT[:, c:c + 128],
                                  probT[:, j * 128 + 32 * p:j * 128 + 32 * p + 32])
                last.then_inc(S["y_mm"], 1)
                pe.wait_ge(S["y"], n + 1)
                mm(p_b[:, :], A("wv"), ysb[:, :]).then_inc(S["c_mm"], 1)
                pe.wait_ge(S["ctxb"], n + 1)
                for e in range(2):
                    mm(p_small[0:D, 32 * e:32 * e + 32], A(f"wo{e}"), ctxb[:, :], start=(e == 0), stop=False)
                    last = mm(p_small[0:D, 32 * e:32 * e + 32], A(f"res{e}"), qsum[:, :], start=False)
                last.then_inc(S["o_mm"], 1)
                pe.wait_ge(S["h1"], n + 1)
                normalise(n, h1T[:, bass.ds(n * SC, SC)], SC)
                project(n, SC)

            pe.wait_ge(s_ca, 16)
            pe.wait_ge(S["weights"], WEIGHTS)
            pe.wait_ge(S["memset"], 4)
            for s in range(2):
                strip(0, s, True)
            with pe.Fori(1, STRIPS // 2) as i:
                for s in range(2):
                    strip(i, s, False)

            pe.wait_ge(S["txt"], 3)
            pe.wait_ge(S["seed_b"], 2 * STRIPS)
            for b in range(B):
                last = pe.transpose(p_x[b // 4][0:D, (b % 4) * 128:(b % 4) * 128 + 128], txt[:, b, :], A("ident"))
            last.then_inc(S["tt_mm"], 1)
            pe.wait_ge(S["tt_copy"], 2)
            with pe.Fori(0, TXT_CHUNKS) as c:
                q = c + LN_TXT
                normalise(q, h1T[:, bass.ds(T_IMG * B + c * CC, CC)], CC)
                pe.wait_ge(S["seed_b"], 2 * q)
                project(q, CC)

            def U(part, net, g):
                return part[:, net * 512 + g * 128:net * 512 + g * 128 + 128]

            def seed(seeds, z_gfi, z_o, dirs, t, first, nothing_before):
                if not nothing_before:
                    pe.wait_ge(S["gates"], t)
                for part in range(2):
                    for d in range(dirs):
                        last = mm(z_gfi(d), ident16[:, :], seeds(part, d, 0, 24), start=(part == 0 and d == 0))
                if first:
                    last.then_inc(S["zgfi"], 1)
                if not nothing_before:
                    pe.wait_ge(S["ogate"], t)
                for part in range(2):
                    for d in range(dirs):
                        last = mm(z_o(d), ident16[:, :], seeds(part, d, 24, 32), start=(part == 0 and d == 0))
                if first:
                    last.then_inc(S["zo"], 1)

            def recur(nets, z_gfi, z_o, t):
                z = lambda g, d: z_o(d) if g == 3 else z_gfi(d)[:, g, :]
                pe.wait_ge(S["ha"], t)
                for g in range(4):
                    for d, net in enumerate(nets):
                        for part in (Ua, Ul):
                            mm(z(g, d), U(part, net, g), ha[:, 8 * d:8 * d + 8], start=False)
                pe.wait_ge(S["hb"], t)
                for g in range(4):
                    for d, net in enumerate(nets):
                        last = mm(z(g, d), U(Ua, net, g), hb[:, 8 * d:8 * d + 8], start=False)
                    if g >= 2:
                        last.then_inc(S["zgfi"] if g == 2 else S["zo"], 1)

            def z_gfi(d):
                return zA[:, 0:48].rearrange("p (g e b) -> p g e b", g=3, e=2)[:, :, d, :]

            def z_o(d):
                return zB[:, 8 * d:8 * d + 8]

            def enc_step(t, first):
                def seeds(part, d, lo, hi):
                    at_ = t * 32 if d == 0 else (2 * T - 1) * 32 - t * 32
                    return XW[part][:, bass.ds(at_ + lo, hi - lo)]
                seed(seeds, z_gfi, z_o, 2, t, first, first)
                if not first:
                    recur((0, 1), z_gfi, z_o, t)

            pe.wait_ge(S["seed_b"], 2 * (STRIPS + TXT_CHUNKS))
            enc_step(0, True)
            enc_step(1, False)
            with pe.Fori(1, T // 2) as i:
                for u in range(2):
                    enc_step(2 * i + u, False)

            pe.wait_ge(S["hb"], T)
            for g in range(4):
                for d in range(2):
                    last = mm(p_t[:, 8 * g:8 * g + 8], A(f"Wd{d}")[:, g * 128:g * 128 + 128], H[:, 8 * d:8 * d + 8],
                              start=(g == 0 and d == 0))
            last.then_inc(S["lat"], 1)
            pe.wait_ge(S["zcs"], 2)

            def dec_step(t, first):
                seed(lambda part, d, lo, hi: zcs[part][:, lo:hi], z_gfi, z_o, 1, t, first, False)
                if not first:
                    recur((2,), z_gfi, z_o, t)

            dec_step(T, True)
            dec_step(T + 1, False)
            with pe.Fori(1, T // 2) as i:
                for u in range(2):
                    dec_step(2 * i + (T + u), False)
            pe.wait_ge(S["hist"], T)

            with pe.Fori(0, CHUNKS) as k:
                mm(p_t[0:D, 0:CC], A("Wo"), hist[:, bass.ds(k * CC, CC)]).then_inc(S["f_mm"], 1)
                pe.wait_ge(S["h2"], k + 1)
                normalise(k + LN_OUT, h2[:, :], CC)
                pe.wait_ge(S["xn"], k + (LN_OUT + 1))
                mm(p_a[:, 0:CC], Bc("wr", 65), xn[:, :]).then_inc(S["r_mm"], 1)
                for h in range(2):
                    last = mm(p_b[:, h * 128:h * 128 + 128], Bc("w1", 65)[:, h * 128:h * 128 + 128], xn[:, :])
                last.then_inc(S["u_mm"], 1)
                pe.wait_ge(S["ug"], k + 1)
                mm(p_t[:, 128:256], A("w2a"), ug[:, 0:128], stop=False)
                mm(p_t[:, 128:256], A("w2b"), ug[:, 128:256], start=False).then_inc(S["y2_mm"], 1)
                pe.wait_ge(S["at"], k + 1)
                pe.wait_ge(S["bt"], k + 1)
                pe.transpose(p_a[:, 256:384], parts[:, :], A("ident")).then_inc(S["ab_mm"], 1)
                pe.wait_ge(S["ab"], k + 1)

            rivals = wrow[0:1, :].rearrange("p (h t b) -> p h t b", h=2, b=B)
            for hf in range(2):
                for b in range(B):
                    last = pe.transpose(p_t[0:HALF, 8 * hf + b:8 * hf + b + 1], rivals[:, hf, :, b], A("ident", 1)[:, 0:1])
            last.then_inc(S["wc_mm"], 1)
            pe.wait_ge(S["beats"], 6)
            for k in range(CHUNKS):
                ih, c = k // (CHUNKS // 2), (k % (CHUNKS // 2)) * CC
                for m, part in enumerate((beats[0][ih], beats[1][ih], tie[ih])):
                    last = mm(p_small[:, k:k + 1], part[:, c:c + CC], ones16[:, 0:1], start=(k == 0 and m == 0))
            last.then_inc(S["rank"], 1)

        @block.scalar
        def _(act):
            def square(q, n):
                act.wait_ge(S["cen"], q + 1)
                act.activation(sq[:, 0:n], p_small[0:D, 0:n], ACT.Square).then_inc(S["sq"], 1)

            def seeds_high(q, t0, nt):
                for d in range(2):
                    act.wait_ge(S["proj"], 2 * q + (d + 1))
                    act.copy(XW[0][:, bass.ds(t0 * 32 + d * T * 32, nt * 32)].rearrange("p (t g b) -> p g t b", g=4, b=B),
                             p_x[d][:, 0:nt * 32].rearrange("p (g t b) -> p g t b", g=4, b=B)).then_inc(S["seed_a"], 1)

            def strip(i, s):
                n = 2 * i + s
                for r in (0, 2):
                    act.wait_ge(S["xt_mm"], 4 * n + (r + 1))
                    act.copy(xT[:, r * 512:r * 512 + 512], p_x[0][:, :]).then_inc(xt_copied[0], 1)
                act.wait_ge(S["qk_mm"], n + 1)
                act.copy(qk[:, :], p_a[:, :]).then_inc(S["qk"], 1)
                act.wait_ge(S["negmax"], n + 1)
                for j in range(4):
                    c = j * 128
                    last = act.activation(prob[:, c:c + 128], score[:, c:c + 128], ACT.Exp, bias=negmax[:, j:j + 1],
                                          accum_out=esum[:, j:j + 1])
                last.then_inc(S["exp"], 1)
                act.wait_ge(S["pt_mm"], n + 1)
                act.copy(probT[:, :], p_b[:, :]).then_inc(S["pt"], 1)
                act.wait_ge(S["y_mm"], n + 1)
                act.copy(ysb[:, :], p_a[:, :]).then_inc(S["y"], 1)
                square(n, SC)
                seeds_high(n, n * GS, GS)

            for s in range(2):
                strip(0, s)
            with act.Fori(1, STRIPS // 2) as i:
                for s in range(2):
                    strip(i, s)
            with act.Fori(0, TXT_CHUNKS) as c:
                square(c + LN_TXT, CC)
                seeds_high(c + LN_TXT, c * CH_T + T_IMG, CH_T)

            def step(t, par, nb):
                act.wait_ge(S["zgfi"], t + 1)
                act.activation(G[:, par, 1:4, 0:nb], zA[:, 0:48].rearrange("p (g b) -> p g b", g=3)[:, :, 0:nb],
                               ACT.Tanh, scale=Z_ACT).then_inc(S["gates"], 1)
                act.wait_ge(S["zo"], t + 1)
                act.activation(G[:, par, 4, 0:nb], zB[:, 0:nb], ACT.Tanh, scale=Z_ACT).then_inc(S["ogate"], 1)
                act.wait_ge(S["cell"], t + 1)
                act.activation(tc[:, 0:nb], G[:, 1 - par, 0, 0:nb], ACT.Tanh, scale=0.5).then_inc(S["tanhc"], 1)

            for t0, nb in ((0, 16), (T, 8)):
                with act.Fori(0, T // 2) as i:
                    for u in range(2):
                        step(2 * i + (t0 + u), u, nb)

            with act.Fori(0, CHUNKS) as k:
                square(k + LN_OUT, CC)
                act.wait_ge(S["r_mm"], k + 1)
                act.copy(wrow[:, bass.ds(k * CC, CC)], p_a[:, 0:CC]).then_inc(S["wrow"], 1)
                act.wait_ge(S["u_mm"], k + 1)
                act.activation(usq[:, :], p_b[:, 0:256], ACT.Square).then_inc(S["usq"], 1)
                act.wait_ge(S["uin2"], k + 1)
                act.activation(uth[:, :], uin2[:, :], ACT.Tanh, scale=GELU_S).then_inc(S["uth"], 1)
                act.wait_ge(S["ab_mm"], k + 1)
                act.copy(ab[:, bass.ds(k * 128, 128)], p_a[:, 256:384]).then_inc(S["ab"], 1)

        @block.vector
        def _(v):
            done = [0]

            def h_(ins):
                done[0] += 1
                ins.then_inc(S["hash"], 1)
                v.wait_ge(S["hash"], done[0])

            def mod(val, m):
                h_(v.tensor_scalar(hq[:, :], val, 1.0 / m, None, ALU.mult))
                h_(v.scalar_tensor_tensor(val, hq[:, :], -float(m), val, ALU.mult, ALU.add))
                h_(v.tensor_scalar(hm[:, :], val, 0.0, float(m), ALU.is_lt, ALU.mult))
                h_(v.tensor_tensor(val, val, hm[:, :], ALU.add))
                h_(v.tensor_scalar(hm[:, :], val, float(m), -float(m), ALU.is_ge, ALU.mult))
                h_(v.tensor_tensor(val, val, hm[:, :], ALU.add))

            v.wait_ge(s_ids, 16)
            h_(v.tensor_copy(idf[:, :], idx_i[:, :]))
            for k in range(2):
                h_(v.tensor_scalar(hp[:, k * B:k * B + B], idf[:, :], float(HASH_A[k] // DIGIT), None, ALU.mult))
                h_(v.tensor_scalar(hx[:, k * B:k * B + B], idf[:, :], float(HASH_A[k] % DIGIT), float(HASH_B[k]),
                                   ALU.mult, ALU.add))
            mod(hp[:, :], HASH_P)
            h_(v.tensor_scalar(hp[:, :], hp[:, :], float(DIGIT), None, ALU.mult))
            mod(hp[:, :], HASH_P)
            h_(v.tensor_tensor(hp[:, :], hp[:, :], hx[:, :], ALU.add))
            mod(hp[:, :], HASH_P)
            mod(hp[:, :], HASH_M)
            h_(v.tensor_scalar(small[:, :], idf[:, :], float(HASH_IC), None, ALU.is_lt))
            for k in range(2):
                c = slice(k * B, k * B + B)
                h_(v.scalar_tensor_tensor(hx[:, c], hp[:, c], float(HASH_IC), idf[:, :], ALU.add, ALU.subtract))
                h_(v.tensor_tensor(hx[:, c], hx[:, c], small[:, :], ALU.mult))
            h_(v.scalar_tensor_tensor(hp[:, :], hp[:, :], float(HASH_IC), hx[:, :], ALU.add, ALU.subtract))
            v.tensor_copy(hidx[:, :], hp[:, :]).then_inc(S["hidx"], 1)
            v.tensor_scalar(widx[:, :], idf[:, :], float(VOCAB - 1), None, ALU.min).then_inc(S["hidx"], 1)

            wd = [0]

            def w_(ins):
                wd[0] += 1
                ins.then_inc(S["weights"], 1)

            def settle():
                v.wait_ge(S["weights"], wd[0])

            def g_block(ap, n):
                return ap.rearrange("p (n c) -> p n c", n=n)[:, :, 0:128]

            v.wait_ge(s_ca, 16)
            v.wait_ge(s_cb, 16)
            Uall = ca[:, PA["Uf"][0]:PA["Ud"][1]]
            Wdall = ca[:, PA["Wd0"][0]:PA["Wd1"][1]]
            Win = cb[:, PB["Wf"][0]:PB["Wb"][1]]
            w2all = ca[:, PA["w2a"][0]:PA["w2b"][1]]
            w_(v.tensor_scalar(A("wq"), A("wq"), 1.0 / (GS * GS), None, ALU.mult))
            w_(v.tensor_scalar(Win, Win, SEED_SCALE, None, ALU.mult))
            w_(v.tensor_scalar(Uall, Uall, U_SCALE, None, ALU.mult))
            w_(v.tensor_scalar(Wdall, Wdall, SEED_SCALE / H_SCALE, None, ALU.mult))
            w_(v.tensor_scalar(A("bd"), A("bd"), SEED_SCALE, None, ALU.mult))
            w_(v.tensor_scalar(A("Wo"), A("Wo"), 1.0 / H_SCALE, None, ALU.mult))
            w_(v.tensor_scalar(w2all, w2all, 0.5, None, ALU.mult))
            w_(v.tensor_scalar(ident16[:, :], A("ident"), SEED_IDENT, None, ALU.mult))
            settle()
            w_(v.tensor_scalar(g_block(Win, 2), g_block(Win, 2), 2.0, None, ALU.mult))
            w_(v.tensor_scalar(g_block(Uall, 3), g_block(Uall, 3), 2.0, None, ALU.mult))
            w_(v.tensor_scalar(g_block(Wdall, 2), g_block(Wdall, 2), 2.0, None, ALU.mult))
            w_(v.tensor_scalar(A("bd")[:, 0:1], A("bd")[:, 0:1], 2.0, None, ALU.mult))
            settle()
            for m in range(3):
                w_(v.tensor_copy(Ua[:, m * 512:m * 512 + 512], Uall[:, m * 512:m * 512 + 512]))
            settle()
            for m in range(3):
                c = slice(m * 512, m * 512 + 512)
                w_(v.tensor_tensor(Ul[:, c], Uall[:, c], Ua[:, c], ALU.subtract))
            w_(v.tensor_copy(zcs[0][:, 0:2], A("bd")[:, 0:2]))
            assert wd[0] == WEIGHTS

            def whiten(q, n):
                v.wait_ge(S["var"], q + 1)
                v.tensor_scalar(varp[:, 0:n], p_small[0:D, 128:128 + n], EPS, None, ALU.add).then_inc(S["varp"], 1)
                v.wait_ge(S["rstd"], q + 1)
                v.tensor_tensor(xn[0:D, 0:n], p_small[0:D, 0:n], rstd[:, 0:n], ALU.mult).then_inc(S["xn"], 1)

            def seeds_low(q, t0, nt):
                for d in range(2):
                    v.wait_ge(S["seed_a"], 2 * q + (d + 1))
                    at_ = [XW[p][:, bass.ds(t0 * 32 + d * T * 32, nt * 32)].rearrange("p (t g b) -> p g t b", g=4, b=B)
                           for p in range(2)]
                    v.tensor_tensor(at_[1], p_x[d][:, 0:nt * 32].rearrange("p (g t b) -> p g t b", g=4, b=B),
                                    at_[0], ALU.subtract).then_inc(S["seed_b"], 1)

            hm_b = A("headmask").rearrange("p (o m) -> p o m", o=1).broadcast_to([128, 32, 16])

            def strip(i, s):
                n = 2 * i + s
                v.wait_ge(s_x[s], 16 * (i + 1))
                for p in range(PAIRS):
                    last = v.tensor_reduce(qsum[:, p * GS:p * GS + GS],
                                           Xv[s][:, p, :, :].rearrange("q w (g c) -> q g w c", c=GS), AX.XY, ALU.add)
                last.then_inc(S["qsum"], 1)
                for r in (1, 3):
                    v.wait_ge(S["xt_mm"], 4 * n + (r + 1))
                    v.tensor_copy(xT[:, r * 512:r * 512 + 512], p_x[1][:, :]).then_inc(xt_copied[1], 1)
                v.wait_ge(S["qp_mm"], n + 1)
                v.tensor_scalar(qp[:, :], p_small[:, 0:32], A("bq"), float(D // NH) ** -0.5, ALU.add,
                                ALU.mult).then_inc(S["qp"], 1)
                v.wait_ge(S["qp"], n + 1)
                v.tensor_tensor(qm[:, :].rearrange("p (n m) -> p n m", m=16),
                                qp[:, :].rearrange("p (n o) -> p n o", o=1).broadcast_to([128, 32, 16]), hm_b,
                                ALU.mult).then_inc(S["qm"], 1)
                v.wait_ge(S["score_mm"], n + 1)
                v.tensor_tensor(score[:, :], p_b[:, :], A("groupmask"), ALU.add).then_inc(S["score"], 1)
                v.wait_ge(S["score"], n + 1)
                v.tensor_reduce(negmax[:, :], score[:, :].rearrange("p (j m) -> p j m", j=4), AX.X, ALU.max,
                                negate=True).then_inc(S["negmax"], 1)
                v.wait_ge(S["exp"], n + 1)
                v.reciprocal(rsum[:, :], esum[:, :]).then_inc(S["rsum"], 1)
                v.wait_ge(S["rsum"], n + 1)
                pv = prob[:, :].rearrange("p (j m) -> p j m", j=4)
                v.tensor_tensor(pv, pv, rsum[:, :].rearrange("p (j o) -> p j o", o=1).broadcast_to([128, 4, 128]),
                                ALU.mult).then_inc(S["prob"], 1)
                v.wait_ge(S["c_mm"], n + 1)
                v.tensor_tensor(cmask[:, :].rearrange("p (n m) -> p n m", m=16),
                                p_b[:, :].rearrange("p (n m) -> p n m", m=16), hm_b, ALU.mult).then_inc(S["cmask"], 1)
                v.wait_ge(S["cmask"], n + 1)
                v.tensor_reduce(ctxv[:, :], cmask[:, :].rearrange("p (n m) -> p n m", m=16), AX.X,
                                ALU.add).then_inc(S["ctxv"], 1)
                v.wait_ge(S["ctxv"], n + 1)
                v.tensor_scalar(ctxb[:, :], ctxv[:, :], A("bv"), None, ALU.add).then_inc(S["ctxb"], 1)
                v.wait_ge(S["o_mm"], n + 1)
                v.tensor_scalar(h1T[:, bass.ds(n * SC, SC)].rearrange("d (g p e) -> d e p g", p=PAIRS, e=2),
                                p_small[0:D, 0:64].rearrange("d (e p g) -> d e p g", e=2, p=PAIRS),
                                Bc("bo"), None, ALU.add).then_inc(S["h1"], 1)
                whiten(n, SC)
                seeds_low(n, n * GS, GS)

            for s in range(2):
                strip(0, s)
            with v.Fori(1, STRIPS // 2) as i:
                for s in range(2):
                    strip(i, s)

            v.wait_ge(S["gath"], 24 * 16)
            for k in range(2):
                v.tensor_tensor(emb[:, k, :, :], emb[:, k, :, :],
                                hwt[:, :, k:k + 1].broadcast_to([128, B, D]), ALU.mult).then_inc(S["txt"], 1)
            v.wait_ge(S["txt"], 2)
            v.tensor_tensor(txt[:, :, :], emb[:, 0, :, :], emb[:, 1, :, :], ALU.add).then_inc(S["txt"], 1)
            v.wait_ge(S["tt_mm"], 1)
            tcols = h1T[:, T_IMG * B:TOK].rearrange("d (t b) -> d b t", b=B)
            for h in range(2):
                v.tensor_copy(tcols[:, 4 * h:4 * h + 4, :],
                              p_x[h][0:D, :].rearrange("d (b t) -> d b t", b=4)).then_inc(S["tt_copy"], 1)
            with v.Fori(0, TXT_CHUNKS) as c:
                whiten(c + LN_TXT, CC)
                seeds_low(c + LN_TXT, c * CH_T + T_IMG, CH_T)

            def step(t, par, nb, keep_at):
                v.wait_ge(S["gates"], t + 1)
                v.scalar_tensor_tensor(prod[:, :, 0:nb], G[:, par, 2:4, 0:nb], 1.0, G[:, par, 0:2, 0:nb], ALU.add,
                                       ALU.mult).then_inc(S["prod"], 1)
                v.wait_ge(S["prod"], t + 1)
                v.scalar_tensor_tensor(G[:, 1 - par, 0, 0:nb], prod[:, 0, 0:nb], 0.5, prod[:, 1, 0:nb], ALU.mult,
                                       ALU.add).then_inc(S["cell"], 1)
                v.wait_ge(S["ogate"], t + 1)
                v.tensor_scalar(osc[:, 0:nb], G[:, par, 4, 0:nb], 1.0, 0.5 * H_SCALE, ALU.add,
                                ALU.mult).then_inc(S["osc"], 1)
                v.wait_ge(S["osc"], t + 1)
                v.wait_ge(S["tanhc"], t + 1)
                v.tensor_tensor(ha[:, 0:nb], osc[:, 0:nb], tc[:, 0:nb], ALU.mult).then_inc(S["ha"], 1)
                v.tensor_tensor(H[:, 0:nb], osc[:, 0:nb], tc[:, 0:nb], ALU.mult).then_inc(S["hfull"], 1)
                v.wait_ge(S["hfull"], t + 1)
                v.tensor_tensor(hb[:, 0:nb], H[:, 0:nb], ha[:, 0:nb], ALU.subtract).then_inc(S["hb"], 1)
                if keep_at is not None:
                    v.tensor_copy(hist[:, bass.ds(keep_at * B, B)], H[:, 0:nb]).then_inc(S["hist"], 1)

            v.wait_ge(S["memset"], 4)
            with v.Fori(0, T // 2) as i:
                for u in range(2):
                    step(2 * i + u, u, 16, None)
            v.wait_ge(S["lat"], 1)
            v.tensor_tensor(zc[:, :].rearrange("p (g b) -> p g b", g=4), p_t[:, 0:32].rearrange("p (g b) -> p g b", g=4),
                            A("bd").rearrange("p (g o) -> p g o", o=1).broadcast_to([128, 4, B]), ALU.add).then_inc(S["zc"], 1)
            v.memset(G[:, 0, 0, :], 0.0).then_inc(S["zc"], 1)
            v.wait_ge(S["zc"], 2)
            v.tensor_copy(zcs[0][:, :], zc[:, :]).then_inc(S["zcs"], 1)
            v.wait_ge(S["zcs"], 1)
            v.tensor_tensor(zcs[1][:, :], zc[:, :], zcs[0][:, :], ALU.subtract).then_inc(S["zcs"], 1)
            with v.Fori(0, T // 2) as i:
                for u in range(2):
                    step(2 * i + (T + u), u, B, 2 * i + u)

            with v.Fori(0, CHUNKS) as k:
                v.wait_ge(S["f_mm"], k + 1)
                v.scalar_tensor_tensor(h2[:, :], p_t[0:D, 0:CC], Bc("boA"), h1T[:, bass.ds(k * CC, CC)], ALU.add,
                                       ALU.add).then_inc(S["h2"], 1)
                whiten(k + LN_OUT, CC)
                v.wait_ge(S["xn"], k + (LN_OUT + 1))
                v.tensor_tensor(parts[0:D, :], h2[:, :], xn[0:D, :], ALU.add).then_inc(S["at"], 1)
                v.wait_ge(S["usq"], k + 1)
                v.tensor_scalar(uin[:, :], usq[:, :], GELU_C, 1.0, ALU.mult, ALU.add).then_inc(S["uin"], 1)
                v.wait_ge(S["uin"], k + 1)
                v.tensor_tensor(uin2[:, :], uin[:, :], p_b[:, 0:256], ALU.mult).then_inc(S["uin2"], 1)
                v.wait_ge(S["uth"], k + 1)
                v.scalar_tensor_tensor(ug[:, :], uth[:, :], 1.0, p_b[:, 0:256], ALU.add, ALU.mult).then_inc(S["ug"], 1)
                v.wait_ge(S["wrow"], k + 1)
                v.wait_ge(S["y2_mm"], k + 1)
                v.scalar_tensor_tensor(parts[D:128, :], p_t[D:128, 128:256], A("b2")[D:128, :], wrow[D:128, bass.ds(k * CC, CC)], ALU.add,
                                       ALU.mult).then_inc(S["bt"], 1)

            v.wait_ge(S["wc_mm"], 1)
            v.tensor_copy(wcol[:, :], p_t[0:HALF, 0:16]).then_inc(S["wcol"], 1)
            v.wait_ge(S["wcol"], 1)

            def own(i):
                return wrow[0:HALF, i * HALF * B:(i + 1) * HALF * B].rearrange("p (t b) -> p t b", b=B)

            def rival(j):
                return wcol[:, 8 * j:8 * j + 8].rearrange("p (o b) -> p o b", o=1).broadcast_to([HALF, HALF, B])

            def tb(ap):
                return ap[:, :].rearrange("p (t b) -> p t b", b=B)

            for j in range(2):
                v.tensor_tensor(tb(equal[j]), own(j), rival(j), ALU.is_equal).then_inc(S["equal"], 1)
            for j in range(2):
                for i in range(2):
                    v.tensor_tensor(tb(beats[j][i]), own(i), rival(j), ALU.is_le if j < i else ALU.is_lt
                                    ).then_inc(S["beats"], 1)
            v.wait_ge(S["equal"], 2)
            for j in range(2):
                v.tensor_tensor(tb(tie[j]), tb(equal[j]),
                                A("before", HALF).rearrange("p (t o) -> p t o", o=1).broadcast_to([HALF, HALF, B]),
                                ALU.mult).then_inc(S["beats"], 1)
            v.wait_ge(S["rank"], 1)
            v.tensor_scalar(keep[:, :], p_small[:, 0:CHUNKS], KEEP - 0.5, None, ALU.is_lt).then_inc(S["keep"], 1)
            v.wait_ge(S["keep"], 1)
            abv = ab[:, :].rearrange("p (k s d) -> p k s d", k=CHUNKS, s=2)
            for c in range(4):
                k = slice(3 * c, 3 * c + 3)
                v.tensor_tensor(routed[:, k, :], abv[:, k, 1, :],
                                keep[:, k].rearrange("p (k o) -> p k o", o=1).broadcast_to([128, 3, D]),
                                ALU.mult).then_inc(S["routed"], 1)
            for c in range(4):
                k = slice(3 * c, 3 * c + 3)
                v.wait_ge(S["routed"], c + 1)
                v.tensor_tensor(fin[:, k, :], routed[:, k, :], abv[:, k, 0, :], ALU.add).then_inc(S["fin"], 1)


def kernel(**inputs):
    import numpy as np
    import concourse.bacc as bacc
    from concourse.bass_utils import run_bass_kernel_spmd

    f = np.float32
    inp = {k: np.asarray(v) for k, v in inputs.items()}
    pa, pb = np.zeros((128, PA_N), f), np.zeros((65, PB_N), f)

    def put(name, val):
        val = np.asarray(val, f)
        pa[:val.shape[0], PA[name][0]:PA[name][1]] = val

    def putb(name, val):
        val = np.asarray(val, f)
        pb[:val.shape[0], PB[name][0]:PB[name][1]] = val

    def diagonal(m):
        z = np.zeros((128, 128), f)
        z[:64, :64] = m
        z[64:, 64:] = m
        return z

    def gates(m):
        m = m.reshape(m.shape[0], 4, HID)
        return np.concatenate([m[:, k] for k in (2, 1, 0, 3)], axis=1)

    def twice(v):
        return np.concatenate([v, v])[:, None]

    eye = np.eye(128, dtype=f)
    put("ident", eye)
    put("wq", diagonal(inp["L0_tok_Wq"].T))
    put("wk", diagonal(inp["L0_tok_Wk"]))
    put("wv", diagonal(inp["L0_tok_Wv"].T))
    for e in range(2):
        wo, res = np.zeros((128, D), f), np.zeros((128, D), f)
        wo[64 * e:64 * e + 64] = inp["L0_tok_Wo"].T
        res[64 * e:64 * e + 64] = np.eye(D, dtype=f) / (GS * GS)
        put(f"wo{e}", wo)
        put(f"res{e}", res)
    q, c = np.arange(128)[:, None], np.arange(16)[None]
    put("headmask", (q // 64 == c // 8) & (q % 64 // 8 == c % 8))
    row, pix = np.arange(128)[:, None], np.arange(512)[None]
    put("groupmask", np.where(row // 16 % 2 == pix % 16 // 8, 0.0, NEG))
    put("bq", twice(inp["L0_tok_bq"]))
    put("bv", twice(inp["L0_tok_bv"]))
    for n in "fbd":
        put("U" + n, gates(inp["L0_attn_U" + n]))
    wd = gates(inp["L0_attn_Wd"])
    put("Wd0", wd[:HID])
    put("Wd1", wd[HID:])
    put("bd", gates(inp["L0_attn_bd"][None]).reshape(4, HID).T)
    put("Wo", inp["L0_attn_Wo"])
    put("w2a", np.pad(inp["L0_ffn_w2"][:128], ((0, 0), (D, 0))))
    put("w2b", np.pad(inp["L0_ffn_w2"][128:], ((0, 0), (D, 0))))
    put("before", np.arange(HALF)[:, None] < np.arange(HALF)[None])
    putb("center", np.tile(np.eye(D) - 1.0 / D, 2))
    putb("mean", np.full((D, 128), 1.0 / D))
    putb("bo", inp["L0_tok_bo"][:, None])
    putb("boA", inp["L0_attn_bo"][:, None])
    put("b2", twice(inp["L0_ffn_b2"]))
    for n, b in (("Wf", "bf"), ("Wb", "bb")):
        putb(n, gates(np.concatenate([inp["L0_attn_" + n], inp["L0_attn_" + b][None]])))
    putb("w1", np.concatenate([inp["L0_ffn_w1"], inp["L0_ffn_b1"][None]]))
    putb("wr", np.repeat(np.concatenate([inp["L0_ffn_wr"], inp["L0_ffn_br"][None]]), 128, axis=1))

    arrays = {
        "x": np.ascontiguousarray(inp["x"]),
        "ids": np.ascontiguousarray(inp["x_txt"].T),
        "table": np.ascontiguousarray(inp["L0_txt_shared_embedding"]),
        "hashw": np.ascontiguousarray(inp["L0_txt_hash_weights_table"]),
        "packa": pa, "packb": pb,
    }
    nc = bacc.Bacc("TRN2", target_bir_lowering=False, num_devices=1)
    aps = [nc.dram_tensor(n, a.shape, mybir.dt.from_np(a.dtype), kind="ExternalInput").ap() for n, a in arrays.items()]
    out = nc.dram_tensor("out", (TOK, D), F32, kind="ExternalOutput").ap()
    build(nc, *aps, out)
    r = run_bass_kernel_spmd(nc, [arrays], core_ids=[0])
    got = r.results[0]["out"].reshape(T, B, D)
    return np.ascontiguousarray(got.transpose(1, 0, 2))
```

```python
from contextlib import ExitStack

import concourse.bass as bass
from concourse import mybir

F32 = mybir.dt.float32
F16 = mybir.dt.float16
BF16 = mybir.dt.bfloat16
I32 = mybir.dt.int32
ALU = mybir.AluOpType
ACT = mybir.ActivationFunctionType
AX = mybir.AxisListType

B, D, W = 8, 64, 64
GS, NH = 8, 8
T_IMG, T_TXT = (W // GS) ** 2, 128
T = T_IMG + T_TXT
HID = 128
PAIRS = B // 2
STRIPS = W // GS
SC = GS * B
TOK = T * B
CH_T = 16
CC = CH_T * B
CHUNKS = T // CH_T
TXT_CHUNKS = T_TXT // CH_T
HALF = T // 2
KEEP = max(1, int(0.5 * T)) - 1
EPS = 1e-5

HASH_P, HASH_M, HASH_IC = 100003, 12500, 4
HASH_A = (12345, 20011)
HASH_B = (6789, 54321)
VOCAB = 25000
DIGIT = 128

H_SCALE = 2.0 ** 15
U_SCALE = 2.0 ** 4
SEED_SCALE = 2.0 ** 5
SEED_IDENT = H_SCALE * U_SCALE / SEED_SCALE
Z_ACT = 0.5 / (H_SCALE * U_SCALE)
NEG = -30000.0
ROOT_MAGIC = float(0x5f3759df)
GELU_C, GELU_S = 0.044715, 0.7978845608028654

PA = {}
_at = 0
for _name, _n in (("ident", 128), ("wq", 128), ("wk", 128), ("wv", 128), ("wo0", D), ("wo1", D), ("res0", D), ("res1", D),
                  ("headmask", 16), ("groupmask", 512), ("bq", 1), ("bv", 1),
                  ("Uf", 512), ("Ub", 512), ("Ud", 512), ("Wd0", 512), ("Wd1", 512), ("bd", 4),
                  ("Wo", D), ("w2a", 128), ("w2b", 128), ("b2", 1), ("before", HALF)):
    PA[_name] = (_at, _at + _n)
    _at += _n
PA_N = _at
PB = {}
_at = 0
for _name, _n in (("center", 128), ("mean", 128), ("bo", 1), ("boA", 1),
                  ("Wf", 512), ("Wb", 512), ("w1", 256), ("wr", 128)):
    PB[_name] = (_at, _at + _n)
    _at += _n
PB_N = _at


def build(nc, x, ids, table, hashw, packa, packb, out):
    with ExitStack() as ctx:
        def sb(name, shape, dt=F32):
            return ctx.enter_context(nc.sbuf_tensor(name, shape, dt))

        def psum(name):
            return ctx.enter_context(nc.psum_tensor(name, [128, 512], F32))

        def sem(name):
            return ctx.enter_context(nc.semaphore(name))

        ca = sb("ca", [128, PA_N])
        cb = sb("cb", [65, PB_N])

        def A(name, rows=128):
            return ca[0:rows, PA[name][0]:PA[name][1]]

        def Bc(name, rows=D):
            return cb[0:rows, PB[name][0]:PB[name][1]]

        X = sb("X", [128, 2, PAIRS * GS * W])
        Xv = [X[:, s, :].rearrange("q (p w h) -> q p w h", p=PAIRS, w=GS) for s in range(2)]
        Xr = sb("Xr", [128, 2, PAIRS, 4, 128])
        qsum = sb("qsum", [128, PAIRS * GS])
        qp = sb("qp", [128, PAIRS * GS])
        qm = sb("qm", [128, PAIRS * GS * 16])
        qk = sb("qk", [128, PAIRS * GS * 16])
        score = sb("score", [128, 512])
        negmax = sb("negmax", [128, 4])
        esum = sb("esum", [128, 4])
        rsum = sb("rsum", [128, 4])
        prob = sb("prob", [128, 512])
        xT = sb("xT", [128, PAIRS * 4 * 128])
        probT = sb("probT", [128, 512])
        ysb = sb("ysb", [128, 512])
        cmask = sb("cmask", [128, 512])
        ctxv = sb("ctxv", [128, PAIRS * GS])
        ctxb = sb("ctxb", [128, PAIRS * GS])
        h1T = sb("h1T", [D, TOK])

        idx_i = sb("idx_i", [128, B], I32)
        idf = sb("idf", [128, B])
        hp = sb("hp", [128, 2 * B])
        hx = sb("hx", [128, 2 * B])
        hq = sb("hq", [128, 2 * B], I32)
        hm = sb("hm", [128, 2 * B])
        small = sb("small", [128, B])
        hidx = sb("hidx", [128, 2 * B], I32)
        widx = sb("widx", [128, B], I32)
        emb = sb("emb", [128, 2, B, D])
        hwt = sb("hwt", [128, B, 2])
        txt = sb("txt", [128, B, D])

        sqT = sb("sqT", [D, TOK])
        vcol, vhalf, rcol, rtmp = [sb(n, [128, CHUNKS]) for n in ("vcol", "vhalf", "rcol", "rtmp")]
        xnT = sb("xnT", [65, TOK])
        seeds = [sb(f"seeds{p}", [128, 2 * CH_T * 32], F16) for p in range(2)]

        ident16 = sb("ident16", [128, 128], F16)
        Ua = sb("Ua", [128, 3 * 512], F16)
        Ul = sb("Ul", [128, 3 * 512], F16)
        G = sb("G", [128, 2, 5, 16])
        prod = sb("prod", [128, 2, 16])
        osc = sb("osc", [128, 16])
        tc = sb("tc", [128, 16])
        H = sb("H", [128, 16])
        ha = sb("ha", [128, 16], F16)
        hb = sb("hb", [128, 16], F16)
        zc = sb("zc", [128, 32])
        zcs = [sb(f"zcs{p}", [128, 32], F16) for p in range(2)]
        hist = sb("hist", [128, CC])
        sq = sb("sq", [D, CC])
        var, var_nh, rstd, rt, ru = [sb(n, [D, CC]) for n in ("var", "var_nh", "rstd", "rt", "ru")]
        three_half = sb("three_half", [D, CC])
        xn = sb("xn", [65, CC])

        h2 = sb("h2", [D, CC])
        wrow = sb("wrow", [128, TOK])
        usq = sb("usq", [128, 256])
        uin = sb("uin", [128, 256])
        uin2 = sb("uin2", [128, 256])
        uth = sb("uth", [128, 256])
        ug = sb("ug", [128, 256])
        parts = sb("parts", [128, CC])
        ab = sb("ab", [128, CHUNKS * 128])
        wcol = sb("wcol", [HALF, 2 * B])
        beats = [[sb(f"beats{j}{i}", [HALF, HALF * B], BF16) for i in range(2)] for j in range(2)]
        equal = [sb(f"equal{j}", [HALF, HALF * B], BF16) for j in range(2)]
        tie = [sb(f"tie{j}", [HALF, HALF * B], BF16) for j in range(2)]
        ones16 = sb("ones16", [HALF, 2], BF16)
        keep = sb("keep", [128, CHUNKS])
        routed = sb("routed", [128, CHUNKS, D])
        fin = sb("fin", [128, CHUNKS, D])

        zA, zB, p_small, p_a, p_b, p_x0, p_x1, p_t = [psum(n) for n in (
            "zA", "zB", "p_small", "p_a", "p_b", "p_x0", "p_x1", "p_t")]
        p_x = [p_x0, p_x1]

        s_ca, s_cb, s_ids = sem("s_ca"), sem("s_cb"), sem("s_ids")
        s_x = [sem("s_x0"), sem("s_x1")]
        xt_copied = [sem("xt_copied0"), sem("xt_copied1")]
        S = {n: sem("s_" + n) for n in (
            "xr qsum qp_mm qp qm qk_mm qk score_mm score negmax exp rsum prob xt_mm pt_mm pt y_mm y c_mm cmask ctxv ctxb "
            "o_mm h1 cen sq var root bc_mm xnT proj seed_a seed_b hash hidx gath txt tt_mm tt_copy weights memset "
            "zgfi zo gates ogate prod cell osc tanhc ha hfull hb first_h lat zc zcs "
            "f_mm h2 fcen fsq fvar varp vseed newton rstd xn "
            "r_mm wrow u_mm usq uin uin2 uth ug y2_mm bt at ab_mm ab wc_mm wcol equal beats rank keep routed fin out"
        ).split()}

        block = ctx.enter_context(nc.Block())
        x_dram = x.rearrange("(p two) c (g w) h -> g (two c) p (w h)", two=2, w=GS)

        WEIGHTS = 19
        ROOTS = 13

        c_banks, r_banks = (zA, zB, p_a), (p_x0, p_x1, p_t)

        def seed_at(d, u):
            return (d * CH_T + (u if d == 0 else CH_T - 1 - u)) * 32

        def half_tokens(h, d):
            return (h if d == 0 else 1 - h) * CH_T // 2

        def seed_half(part, h, d):
            at_ = (d * CH_T + half_tokens(h, d)) * 32
            return seeds[part][:, at_:at_ + CH_T // 2 * 32].rearrange("p (t g b) -> p g t b", g=4, b=B)

        def proj_half(h, d):
            t0 = half_tokens(h, d)
            return p_x[d][:, :].rearrange("p (g t b) -> p g t b", g=4, b=B)[:, :, t0:t0 + CH_T // 2, :]

        @block.sync
        def _(sp):
            def load_strip(n, s):
                sp.dma_start(X[:, s, :].rearrange("q (p n) -> q p n", p=PAIRS),
                             x_dram[bass.ds(n, 1)].rearrange("g q p n -> (g q) p n")).then_inc(s_x[s], 16)
            sp.dma_start(idx_i[:, :], ids).then_inc(s_ids, 16)
            load_strip(0, 0)
            sp.dma_start(ca[:, :], packa).then_inc(s_ca, 16)
            sp.dma_start(cb[:, :], packb).then_inc(s_cb, 16)
            load_strip(1, 1)
            with sp.Fori(1, STRIPS // 2) as i:
                for s in range(2):
                    sp.wait_ge(S["qsum"], 2 * i + s - 1)
                    sp.wait_ge(S["xr"], 2 * i + s - 1)
                    load_strip(2 * i + s, s)
            for c in range(4):
                sp.wait_ge(S["fin"], c + 1)
                k0, k1 = 3 * c, 3 * c + 3
                sp.dma_start(out[k0 * CC:k1 * CC, :].rearrange("(k p) d -> p k d", p=128),
                             fin[:, k0:k1, :]).then_inc(S["out"], 16)
            sp.wait_ge(S["out"], 64)

        @block.gpsimd
        def _(pool):
            pool.memset(G[:, :, 0:4, :], 0.0).then_inc(S["gates"], 1)
            pool.memset(G[:, :, 4, :], 0.0).then_inc(S["ogate"], 1)
            pool.memset(ha[:, :], 0.0).then_inc(S["ha"], 1)
            pool.memset(hb[:, :], 0.0).then_inc(S["hb"], 1)
            pool.memset(three_half[:, :], 1.5).then_inc(S["memset"], 1)
            pool.memset(ones16[:, :], 1.0).then_inc(S["memset"], 1)
            pool.wait_ge(S["memset"], 2)
            pool.memset(xn[64:65, :], 1.0).then_inc(S["memset"], 1)
            pool.memset(xnT[64:65, :], 1.0).then_inc(S["memset"], 1)
            pool.wait_ge(S["memset"], 4)
            pool.wait_ge(S["hidx"], 2)
            for b in range(B):
                for k in range(2):
                    pool.indirect_dma_start(
                        out=emb[:, k, b, :], out_offset=None, in_=table,
                        in_offset=bass.IndirectOffsetOnAxis(ap=hidx[:, k * B + b:k * B + b + 1], axis=0)
                    ).then_inc(S["gath"], 16)
                pool.indirect_dma_start(
                    out=hwt[:, b, :], out_offset=None, in_=hashw,
                    in_offset=bass.IndirectOffsetOnAxis(ap=widx[:, b:b + 1], axis=0)
                ).then_inc(S["gath"], 16)

            def newton(k):
                pool.wait_ge(S["vseed"], k + 1)
                for r in range(3):
                    for m, (o, a, b, op) in enumerate(((rt, rstd, rstd, ALU.mult), (ru, rt, var_nh, ALU.mult),
                                                       (rt, ru, three_half, ALU.add), (rstd, rt, rstd, ALU.mult))):
                        if 4 * r + m > 0:
                            pool.wait_ge(S["newton"], k * 12 + (4 * r + m))
                        pool.tensor_tensor(o[:, :], a[:, :], b[:, :], op).then_inc(S["newton"], 1)

            with pool.Fori(0, CHUNKS) as k:
                newton(k)

        @block.tensor
        def _(pe):
            def mm(o, l, r, start=True, stop=True):
                return pe.matmul(o, l, r, start=start, stop=stop, skip_group_check=True)

            def project(c, d, gates, ahead=False):
                cols = c * CC if d == 0 else (CHUNKS - 1) * CC - c * CC
                for g in gates:
                    last = mm(p_x[d][:, g * CC:g * CC + CC], Bc("Wf" if d == 0 else "Wb", 65)[:, g * 128:g * 128 + 128],
                              xnT[:, bass.ds(cols, CC)])
                if gates[-1] == 3:
                    last.then_inc(S["proj"], 1)

            def strip(i, s, first):
                n = 2 * i + s
                later = not first or s > 0
                pe.wait_ge(S["xr"], n + 1)
                for r in range(PAIRS):
                    if later or r >= 2:
                        pe.wait_ge(xt_copied[r % 2], 2 * n + r // 2)
                    for j in range(4):
                        last = pe.transpose(p_x[r % 2][:, j * 128:j * 128 + 128], Xr[:, s, r, j, :], A("ident"))
                    last.then_inc(S["xt_mm"], 1)
                pe.wait_ge(S["qsum"], n + 1)
                mm(p_small[:, 0:32], A("wq"), qsum[:, :]).then_inc(S["qp_mm"], 1)
                pe.wait_ge(S["qm"], n + 1)
                mm(p_a[:, :], A("wk"), qm[:, :]).then_inc(S["qk_mm"], 1)
                pe.wait_ge(S["qk"], n + 1)
                for p in range(PAIRS):
                    for j in range(4):
                        c = (p * GS + 2 * j) * 16
                        last = mm(p_b[32 * p:32 * p + 32, j * 128:j * 128 + 128], qk[:, c:c + 32], Xr[:, s, p, j, :])
                last.then_inc(S["score_mm"], 1)
                pe.wait_ge(S["prob"], n + 1)
                for j in range(4):
                    last = pe.transpose(p_b[:, j * 128:j * 128 + 128], prob[:, j * 128:j * 128 + 128], A("ident"))
                last.then_inc(S["pt_mm"], 1)
                pe.wait_ge(xt_copied[0], 2 * n + 2)
                pe.wait_ge(xt_copied[1], 2 * n + 2)
                pe.wait_ge(S["pt"], n + 1)
                for p in range(PAIRS):
                    for j in range(4):
                        c = (p * 4 + j) * 128
                        last = mm(p_a[:, (p * 4 + j) * 32:(p * 4 + j) * 32 + 32], xT[:, c:c + 128],
                                  probT[:, j * 128 + 32 * p:j * 128 + 32 * p + 32])
                last.then_inc(S["y_mm"], 1)
                pe.wait_ge(S["y"], n + 1)
                mm(p_b[:, :], A("wv"), ysb[:, :]).then_inc(S["c_mm"], 1)
                pe.wait_ge(S["ctxb"], n + 1)
                for e in range(2):
                    mm(p_small[0:D, 32 * e:32 * e + 32], A(f"wo{e}"), ctxb[:, :], start=(e == 0), stop=False)
                    last = mm(p_small[0:D, 32 * e:32 * e + 32], A(f"res{e}"), qsum[:, :], start=False)
                last.then_inc(S["o_mm"], 1)
                pe.wait_ge(S["h1"], n + 1)

            pe.wait_ge(s_ca, 16)
            pe.wait_ge(S["weights"], WEIGHTS)
            pe.wait_ge(S["memset"], 4)
            for s in range(2):
                strip(0, s, True)
            with pe.Fori(1, STRIPS // 2) as i:
                for s in range(2):
                    strip(i, s, False)

            pe.wait_ge(S["txt"], 3)
            for r in range(2):
                pe.wait_ge(xt_copied[r], 2 * STRIPS)
            for b in range(B):
                last = pe.transpose(p_x[b // 4][0:D, (b % 4) * 128:(b % 4) * 128 + 128], txt[:, b, :], A("ident"))
            last.then_inc(S["tt_mm"], 1)

            for m, bank in enumerate(c_banks):
                if m == 1:
                    pe.wait_ge(S["tt_copy"], 2)
                mm(bank[:, :], Bc("center"), h1T[:, m * 512:m * 512 + 512]).then_inc(S["cen"], 1)
            for m in range(3):
                pe.wait_ge(S["sq"], m + 1)
                for k in range(4 * m, 4 * m + 4):
                    last = mm(p_small[:, k:k + 1], sqT[:, k * CC:k * CC + CC], Bc("mean")[:, 0:1])
            last.then_inc(S["var"], 1)
            pe.wait_ge(S["root"], ROOTS)
            for m, bank in enumerate(r_banks):
                for k in range(4):
                    c = 4 * m + k
                    last = mm(bank[:, k * CC:k * CC + CC], rcol[:, c:c + 1].broadcast_to([128, 128]), A("ident"))
                last.then_inc(S["bc_mm"], 1)
            pe.wait_ge(S["xnT"], 3)
            for d in range(2):
                project(0, d, range(4))

            def U(part, net, g):
                return part[:, net * 512 + g * 128:net * 512 + g * 128 + 128]

            def z_gfi(d):
                return zA[:, 0:48].rearrange("p (g e b) -> p g e b", g=3, e=2)[:, :, d, :]

            def z_o(d):
                return zB[:, 8 * d:8 * d + 8]

            def seed(rows, dirs, t):
                pe.wait_ge(S["gates"], t + 1)
                for part in range(2):
                    for d in range(dirs):
                        mm(z_gfi(d), ident16[:, :], rows(part, d)[:, 0:24], start=(part == 0 and d == 0))
                pe.wait_ge(S["ogate"], t + 1)
                for part in range(2):
                    for d in range(dirs):
                        mm(z_o(d), ident16[:, :], rows(part, d)[:, 24:32], start=(part == 0 and d == 0))

            def recur(nets, t):
                z = lambda g, d: z_o(d) if g == 3 else z_gfi(d)[:, g, :]

                def high(gs):
                    for g in gs:
                        for d, net in enumerate(nets):
                            for part in (Ua, Ul):
                                mm(z(g, d), U(part, net, g), ha[:, 8 * d:8 * d + 8], start=False)

                def low(gs):
                    for g in gs:
                        for d, net in enumerate(nets):
                            last = mm(z(g, d), U(Ua, net, g), hb[:, 8 * d:8 * d + 8], start=False)
                    return last

                pe.wait_ge(S["ha"], t + 1)
                high(range(3))
                if len(nets) == 1:
                    high([3])
                pe.wait_ge(S["hb"], t + 1)
                low(range(3)).then_inc(S["zgfi"], 1)
                if len(nets) == 2:
                    high([3])
                low([3]).then_inc(S["zo"], 1)

            def enc_body(c, ahead):
                for u in range(CH_T):
                    if u % 8 == 0:
                        pe.wait_ge(S["seed_b"], 4 * c + (2 + u // 4))
                    seed(lambda part, d: seeds[part][:, seed_at(d, u):seed_at(d, u) + 32], 2, c * CH_T + u)
                    if ahead and 4 <= u < 12:
                        if u == 4:
                            pe.wait_ge(S["seed_b"], 4 * c + 3)
                        project(c + 1, (u - 4) // 4, [u % 4])
                    recur((0, 1), c * CH_T + u)

            with pe.Fori(0, CHUNKS - 1) as c:
                enc_body(c, True)
            enc_body(CHUNKS - 1, False)

            pe.wait_ge(S["hb"], T + 1)
            for g in range(4):
                for d in range(2):
                    last = mm(p_t[:, 8 * g:8 * g + 8], A(f"Wd{d}")[:, g * 128:g * 128 + 128], H[:, 8 * d:8 * d + 8],
                              start=(g == 0 and d == 0))
            last.then_inc(S["lat"], 1)
            pe.wait_ge(S["zcs"], 2)

            def mlp(u, k):
                if u == 1:
                    mm(p_t[0:D, 0:CC], A("Wo"), hist[:, :]).then_inc(S["f_mm"], 1)
                elif u == 2:
                    pe.wait_ge(S["h2"], k + 1)
                    mm(p_small[:, 0:CC], Bc("center"), h2[:, :]).then_inc(S["fcen"], 1)
                elif u == 3:
                    pe.wait_ge(S["fsq"], k + 1)
                    mm(p_small[:, CC:2 * CC], Bc("mean"), sq[:, :]).then_inc(S["fvar"], 1)
                elif u in (8, 9):
                    h = u - 8
                    pe.wait_ge(S["xn"], k + 1)
                    last = mm(p_b[:, h * 128:h * 128 + 128], Bc("w1", 65)[:, h * 128:h * 128 + 128], xn[:, :])
                    if h == 1:
                        last.then_inc(S["u_mm"], 1)
                elif u == 10:
                    mm(p_a[:, 0:CC], Bc("wr", 65), xn[:, :]).then_inc(S["r_mm"], 1)
                elif u == 13:
                    pe.wait_ge(S["ug"], k + 1)
                    mm(p_x1[:, 0:CC], A("w2a"), ug[:, 0:128], stop=False)
                    mm(p_x1[:, 0:CC], A("w2b"), ug[:, 128:256], start=False).then_inc(S["y2_mm"], 1)
                elif u == 14:
                    pe.wait_ge(S["bt"], k + 1)
                    pe.wait_ge(S["at"], k + 1)
                    pe.transpose(p_x0[:, 0:CC], parts[:, :], A("ident")).then_inc(S["ab_mm"], 1)

            def dec_body(k, behind):
                for u in range(CH_T):
                    seed(lambda part, d: zcs[part][:, :], 1, k * CH_T + (T + u))
                    if behind:
                        mlp(u, k - 1)
                    recur((2,), k * CH_T + (T + u))

            dec_body(0, False)
            with pe.Fori(1, CHUNKS) as k:
                dec_body(k, True)
            pe.wait_ge(S["hb"], 2 * T + 1)
            for u in range(CH_T):
                mlp(u, CHUNKS - 1)
            pe.wait_ge(S["ab"], CHUNKS)

            rivals = wrow[0:1, :].rearrange("p (h t b) -> p h t b", h=2, b=B)
            for hf in range(2):
                for b in range(B):
                    last = pe.transpose(p_t[0:HALF, 8 * hf + b:8 * hf + b + 1], rivals[:, hf, :, b], A("ident", 1)[:, 0:1])
            last.then_inc(S["wc_mm"], 1)
            pe.wait_ge(S["beats"], 6)
            for k in range(CHUNKS):
                ih, c = k // (CHUNKS // 2), (k % (CHUNKS // 2)) * CC
                for m, part in enumerate((beats[0][ih], beats[1][ih], tie[ih])):
                    last = mm(p_small[:, k:k + 1], part[:, c:c + CC], ones16[:, 0:1], start=(k == 0 and m == 0))
            last.then_inc(S["rank"], 1)

        @block.scalar
        def _(act):
            def strip(i, s):
                n = 2 * i + s
                act.wait_ge(s_x[s], 16 * (i + 1))
                for p in range(PAIRS):
                    last = act.copy(Xr[:, s, p, :, :].rearrange("q j (w c) -> q j w c", c=16),
                                    Xv[s][:, p, :, :].rearrange("q w (j c) -> q j w c", c=16))
                last.then_inc(S["xr"], 1)
                for r in (0, 2):
                    act.wait_ge(S["xt_mm"], 4 * n + (r + 1))
                    act.copy(xT[:, r * 512:r * 512 + 512], p_x[0][:, :]).then_inc(xt_copied[0], 1)
                act.wait_ge(S["qk_mm"], n + 1)
                act.copy(qk[:, :], p_a[:, :]).then_inc(S["qk"], 1)
                act.wait_ge(S["negmax"], n + 1)
                for j in range(4):
                    c = j * 128
                    last = act.activation(prob[:, c:c + 128], score[:, c:c + 128], ACT.Exp, bias=negmax[:, j:j + 1],
                                          accum_out=esum[:, j:j + 1])
                last.then_inc(S["exp"], 1)
                act.wait_ge(S["pt_mm"], n + 1)
                act.copy(probT[:, :], p_b[:, :]).then_inc(S["pt"], 1)
                act.wait_ge(S["y_mm"], n + 1)
                act.copy(ysb[:, :], p_a[:, :]).then_inc(S["y"], 1)

            for s in range(2):
                strip(0, s)
            with act.Fori(1, STRIPS // 2) as i:
                for s in range(2):
                    strip(i, s)
            for m, bank in enumerate(c_banks):
                act.wait_ge(S["cen"], m + 1)
                act.activation(sqT[:, m * 512:m * 512 + 512], bank[0:D, :], ACT.Square).then_inc(S["sq"], 1)

            def seeds_high(c, h, d):
                act.wait_ge(S["proj"], 2 * c + (d + 1))
                act.copy(seed_half(0, h, d), proj_half(h, d)).then_inc(S["seed_a"], 1)

            def step(t, par, nb):
                act.wait_ge(S["zgfi"], t + 1)
                act.activation(G[:, par, 1:4, 0:nb], zA[:, 0:48].rearrange("p (g b) -> p g b", g=3)[:, :, 0:nb],
                               ACT.Tanh, scale=Z_ACT).then_inc(S["gates"], 1)
                act.wait_ge(S["zo"], t + 1)
                act.activation(G[:, par, 4, 0:nb], zB[:, 0:nb], ACT.Tanh, scale=Z_ACT).then_inc(S["ogate"], 1)
                act.wait_ge(S["cell"], t + 1)
                act.activation(tc[:, 0:nb], G[:, 1 - par, 0, 0:nb], ACT.Tanh, scale=0.5).then_inc(S["tanhc"], 1)

            def enc_body(c, ahead):
                for u in range(CH_T):
                    step(c * CH_T + u, u % 2, 2 * B)
                    if u in (0, 2):
                        seeds_high(c, 1, u // 2)
                    elif ahead and u in (9, 12):
                        seeds_high(c + 1, 0, (u - 9) // 3)

            for d in range(2):
                seeds_high(0, 0, d)
            with act.Fori(0, CHUNKS - 1) as c:
                enc_body(c, True)
            enc_body(CHUNKS - 1, False)

            def mlp(u, k):
                if u == 2:
                    act.wait_ge(S["fcen"], k + 1)
                    act.activation(sq[:, :], p_small[0:D, 0:CC], ACT.Square).then_inc(S["fsq"], 1)
                elif u == 9:
                    act.wait_ge(S["u_mm"], k + 1)
                    act.activation(usq[:, :], p_b[:, 0:256], ACT.Square).then_inc(S["usq"], 1)
                elif u == 10:
                    act.wait_ge(S["r_mm"], k + 1)
                    act.copy(wrow[:, bass.ds(k * CC, CC)], p_a[:, 0:CC]).then_inc(S["wrow"], 1)
                elif u == 11:
                    act.wait_ge(S["uin2"], k + 1)
                    act.activation(uth[:, :], uin2[:, :], ACT.Tanh, scale=GELU_S).then_inc(S["uth"], 1)
                elif u == 15:
                    act.wait_ge(S["ab_mm"], k + 1)
                    act.copy(ab[:, bass.ds(k * 128, 128)], p_x0[:, 0:CC]).then_inc(S["ab"], 1)

            def dec_body(k, behind):
                for u in range(CH_T):
                    step(k * CH_T + (T + u), u % 2, B)
                    if behind:
                        mlp(u, k - 1)

            dec_body(0, False)
            with act.Fori(1, CHUNKS) as k:
                dec_body(k, True)
            for u in range(CH_T):
                mlp(u, CHUNKS - 1)

        @block.vector
        def _(v):
            done = [0]

            def h_(ins):
                done[0] += 1
                ins.then_inc(S["hash"], 1)
                v.wait_ge(S["hash"], done[0])

            def mod(val, m):
                h_(v.tensor_scalar(hq[:, :], val, 1.0 / m, None, ALU.mult))
                h_(v.scalar_tensor_tensor(val, hq[:, :], -float(m), val, ALU.mult, ALU.add))
                h_(v.tensor_scalar(hm[:, :], val, 0.0, float(m), ALU.is_lt, ALU.mult))
                h_(v.tensor_tensor(val, val, hm[:, :], ALU.add))
                h_(v.tensor_scalar(hm[:, :], val, float(m), -float(m), ALU.is_ge, ALU.mult))
                h_(v.tensor_tensor(val, val, hm[:, :], ALU.add))

            v.wait_ge(s_ids, 16)
            h_(v.tensor_copy(idf[:, :], idx_i[:, :]))
            for k in range(2):
                h_(v.tensor_scalar(hp[:, k * B:k * B + B], idf[:, :], float(HASH_A[k] // DIGIT), None, ALU.mult))
                h_(v.tensor_scalar(hx[:, k * B:k * B + B], idf[:, :], float(HASH_A[k] % DIGIT), float(HASH_B[k]),
                                   ALU.mult, ALU.add))
            mod(hp[:, :], HASH_P)
            h_(v.tensor_scalar(hp[:, :], hp[:, :], float(DIGIT), None, ALU.mult))
            mod(hp[:, :], HASH_P)
            h_(v.tensor_tensor(hp[:, :], hp[:, :], hx[:, :], ALU.add))
            mod(hp[:, :], HASH_P)
            mod(hp[:, :], HASH_M)
            h_(v.tensor_scalar(small[:, :], idf[:, :], float(HASH_IC), None, ALU.is_lt))
            for k in range(2):
                c = slice(k * B, k * B + B)
                h_(v.scalar_tensor_tensor(hx[:, c], hp[:, c], float(HASH_IC), idf[:, :], ALU.add, ALU.subtract))
                h_(v.tensor_tensor(hx[:, c], hx[:, c], small[:, :], ALU.mult))
            h_(v.scalar_tensor_tensor(hp[:, :], hp[:, :], float(HASH_IC), hx[:, :], ALU.add, ALU.subtract))
            v.tensor_copy(hidx[:, :], hp[:, :]).then_inc(S["hidx"], 1)
            v.tensor_scalar(widx[:, :], idf[:, :], float(VOCAB - 1), None, ALU.min).then_inc(S["hidx"], 1)

            wd = [0]

            def w_(ins):
                wd[0] += 1
                ins.then_inc(S["weights"], 1)

            def settle():
                v.wait_ge(S["weights"], wd[0])

            def g_block(ap, n):
                return ap.rearrange("p (n c) -> p n c", n=n)[:, :, 0:128]

            v.wait_ge(s_ca, 16)
            v.wait_ge(s_cb, 16)
            Uall = ca[:, PA["Uf"][0]:PA["Ud"][1]]
            Wdall = ca[:, PA["Wd0"][0]:PA["Wd1"][1]]
            Win = cb[:, PB["Wf"][0]:PB["Wb"][1]]
            w2all = ca[:, PA["w2a"][0]:PA["w2b"][1]]
            w_(v.tensor_scalar(A("wq"), A("wq"), 1.0 / (GS * GS), None, ALU.mult))
            w_(v.tensor_scalar(Win, Win, SEED_SCALE, None, ALU.mult))
            w_(v.tensor_scalar(Uall, Uall, U_SCALE, None, ALU.mult))
            w_(v.tensor_scalar(Wdall, Wdall, SEED_SCALE / H_SCALE, None, ALU.mult))
            w_(v.tensor_scalar(A("bd"), A("bd"), SEED_SCALE, None, ALU.mult))
            w_(v.tensor_scalar(A("Wo"), A("Wo"), 1.0 / H_SCALE, None, ALU.mult))
            w_(v.tensor_scalar(w2all, w2all, 0.5, None, ALU.mult))
            w_(v.tensor_scalar(ident16[:, :], A("ident"), SEED_IDENT, None, ALU.mult))
            settle()
            w_(v.tensor_scalar(g_block(Win, 2), g_block(Win, 2), 2.0, None, ALU.mult))
            w_(v.tensor_scalar(g_block(Uall, 3), g_block(Uall, 3), 2.0, None, ALU.mult))
            w_(v.tensor_scalar(g_block(Wdall, 2), g_block(Wdall, 2), 2.0, None, ALU.mult))
            w_(v.tensor_scalar(A("bd")[:, 0:1], A("bd")[:, 0:1], 2.0, None, ALU.mult))
            settle()
            for m in range(3):
                w_(v.tensor_copy(Ua[:, m * 512:m * 512 + 512], Uall[:, m * 512:m * 512 + 512]))
            settle()
            for m in range(3):
                c = slice(m * 512, m * 512 + 512)
                w_(v.tensor_tensor(Ul[:, c], Uall[:, c], Ua[:, c], ALU.subtract))
            w_(v.tensor_copy(zcs[0][:, 0:2], A("bd")[:, 0:2]))
            assert wd[0] == WEIGHTS

            def seeds_low(c, h, d):
                v.wait_ge(S["seed_a"], 4 * c + (2 * h + d + 1))
                v.tensor_tensor(seed_half(1, h, d), proj_half(h, d), seed_half(0, h, d), ALU.subtract).then_inc(S["seed_b"], 1)

            hm_b = A("headmask").rearrange("p (o m) -> p o m", o=1).broadcast_to([128, 32, 16])

            def strip(i, s):
                n = 2 * i + s
                v.wait_ge(s_x[s], 16 * (i + 1))
                for p in range(PAIRS):
                    last = v.tensor_reduce(qsum[:, p * GS:p * GS + GS],
                                           Xv[s][:, p, :, :].rearrange("q w (g c) -> q g w c", c=GS), AX.XY, ALU.add)
                last.then_inc(S["qsum"], 1)
                for r in (1, 3):
                    v.wait_ge(S["xt_mm"], 4 * n + (r + 1))
                    v.tensor_copy(xT[:, r * 512:r * 512 + 512], p_x[1][:, :]).then_inc(xt_copied[1], 1)
                v.wait_ge(S["qp_mm"], n + 1)
                v.tensor_scalar(qp[:, :], p_small[:, 0:32], A("bq"), float(D // NH) ** -0.5, ALU.add,
                                ALU.mult).then_inc(S["qp"], 1)
                v.wait_ge(S["qp"], n + 1)
                v.tensor_tensor(qm[:, :].rearrange("p (n m) -> p n m", m=16),
                                qp[:, :].rearrange("p (n o) -> p n o", o=1).broadcast_to([128, 32, 16]), hm_b,
                                ALU.mult).then_inc(S["qm"], 1)
                v.wait_ge(S["score_mm"], n + 1)
                v.tensor_tensor(score[:, :], p_b[:, :], A("groupmask"), ALU.add).then_inc(S["score"], 1)
                v.wait_ge(S["score"], n + 1)
                v.tensor_reduce(negmax[:, :], score[:, :].rearrange("p (j m) -> p j m", j=4), AX.X, ALU.max,
                                negate=True).then_inc(S["negmax"], 1)
                v.wait_ge(S["exp"], n + 1)
                v.reciprocal(rsum[:, :], esum[:, :]).then_inc(S["rsum"], 1)
                v.wait_ge(S["rsum"], n + 1)
                pv = prob[:, :].rearrange("p (j m) -> p j m", j=4)
                v.tensor_tensor(pv, pv, rsum[:, :].rearrange("p (j o) -> p j o", o=1).broadcast_to([128, 4, 128]),
                                ALU.mult).then_inc(S["prob"], 1)
                v.wait_ge(S["c_mm"], n + 1)
                v.tensor_tensor(cmask[:, :].rearrange("p (n m) -> p n m", m=16),
                                p_b[:, :].rearrange("p (n m) -> p n m", m=16), hm_b, ALU.mult).then_inc(S["cmask"], 1)
                v.wait_ge(S["cmask"], n + 1)
                v.tensor_reduce(ctxv[:, :], cmask[:, :].rearrange("p (n m) -> p n m", m=16), AX.X,
                                ALU.add).then_inc(S["ctxv"], 1)
                v.wait_ge(S["ctxv"], n + 1)
                v.tensor_scalar(ctxb[:, :], ctxv[:, :], A("bv"), None, ALU.add).then_inc(S["ctxb"], 1)
                v.wait_ge(S["o_mm"], n + 1)
                v.tensor_scalar(h1T[:, bass.ds(n * SC, SC)].rearrange("d (g p e) -> d e p g", p=PAIRS, e=2),
                                p_small[0:D, 0:64].rearrange("d (e p g) -> d e p g", e=2, p=PAIRS),
                                Bc("bo"), None, ALU.add).then_inc(S["h1"], 1)

            for s in range(2):
                strip(0, s)
            with v.Fori(1, STRIPS // 2) as i:
                for s in range(2):
                    strip(i, s)

            v.wait_ge(S["gath"], 24 * 16)
            for k in range(2):
                v.tensor_tensor(emb[:, k, :, :], emb[:, k, :, :],
                                hwt[:, :, k:k + 1].broadcast_to([128, B, D]), ALU.mult).then_inc(S["txt"], 1)
            v.wait_ge(S["txt"], 2)
            v.tensor_tensor(txt[:, :, :], emb[:, 0, :, :], emb[:, 1, :, :], ALU.add).then_inc(S["txt"], 1)
            v.wait_ge(S["tt_mm"], 1)
            tcols = h1T[:, T_IMG * B:TOK].rearrange("d (t b) -> d b t", b=B)
            for h in range(2):
                v.tensor_copy(tcols[:, 4 * h:4 * h + 4, :],
                              p_x[h][0:D, :].rearrange("d (b t) -> d b t", b=4)).then_inc(S["tt_copy"], 1)

            rd = [0]

            def r_(ins):
                rd[0] += 1
                ins.then_inc(S["root"], 1)

            def root():
                v.wait_ge(S["root"], rd[0])

            v.wait_ge(S["var"], 1)
            r_(v.tensor_scalar(vcol[:, :], p_small[:, 0:CHUNKS], EPS, None, ALU.add))
            r_(v.tensor_scalar(vhalf[:, :], p_small[:, 0:CHUNKS], EPS, -0.5, ALU.add, ALU.mult))
            root()
            r_(v.tensor_scalar(rtmp[:, :].bitcast(I32), vcol[:, :].bitcast(I32), 1, None, ALU.logical_shift_right))
            root()
            r_(v.tensor_scalar(rcol[:, :].bitcast(I32), rtmp[:, :].bitcast(I32), -1.0, ROOT_MAGIC, ALU.mult, ALU.add))
            root()
            for _ in range(3):
                r_(v.tensor_tensor(rtmp[:, :], rcol[:, :], rcol[:, :], ALU.mult))
                root()
                r_(v.tensor_tensor(rtmp[:, :], rtmp[:, :], vhalf[:, :], ALU.mult))
                root()
                r_(v.scalar_tensor_tensor(rcol[:, :], rtmp[:, :], 1.5, rcol[:, :], ALU.add, ALU.mult))
                root()
            assert rd[0] == ROOTS
            for m in range(3):
                v.wait_ge(S["bc_mm"], m + 1)
                v.tensor_copy(sqT[:, m * 512:m * 512 + 512], r_banks[m][0:D, :]).then_inc(S["first_h"], 1)
                v.wait_ge(S["first_h"], m + 1)
                v.tensor_tensor(xnT[0:D, m * 512:m * 512 + 512], c_banks[m][0:D, :], sqT[:, m * 512:m * 512 + 512],
                                ALU.mult).then_inc(S["xnT"], 1)

            def step(t, par, nb, h_out):
                v.wait_ge(S["gates"], t + 2)
                v.scalar_tensor_tensor(prod[:, :, 0:nb], G[:, par, 2:4, 0:nb], 1.0, G[:, par, 0:2, 0:nb], ALU.add,
                                       ALU.mult).then_inc(S["prod"], 1)
                v.wait_ge(S["prod"], t + 1)
                v.scalar_tensor_tensor(G[:, 1 - par, 0, 0:nb], prod[:, 0, 0:nb], 0.5, prod[:, 1, 0:nb], ALU.mult,
                                       ALU.add).then_inc(S["cell"], 1)
                v.wait_ge(S["ogate"], t + 2)
                v.tensor_scalar(osc[:, 0:nb], G[:, par, 4, 0:nb], 1.0, 0.5 * H_SCALE, ALU.add,
                                ALU.mult).then_inc(S["osc"], 1)
                v.wait_ge(S["tanhc"], t + 1)
                v.wait_ge(S["osc"], t + 1)
                v.tensor_tensor(ha[:, 0:nb], osc[:, 0:nb], tc[:, 0:nb], ALU.mult).then_inc(S["ha"], 1)
                v.tensor_tensor(h_out, osc[:, 0:nb], tc[:, 0:nb], ALU.mult).then_inc(S["hfull"], 1)
                v.wait_ge(S["hfull"], t + 1)
                v.tensor_tensor(hb[:, 0:nb], h_out, ha[:, 0:nb], ALU.subtract).then_inc(S["hb"], 1)

            def enc_body(c, ahead):
                for u in range(CH_T):
                    step(c * CH_T + u, u % 2, 2 * B, H[:, :])
                    if u in (1, 3):
                        seeds_low(c, 1, u // 2)
                    elif ahead and u in (10, 13):
                        seeds_low(c + 1, 0, (u - 10) // 3)

            v.wait_ge(S["memset"], 4)
            for d in range(2):
                seeds_low(0, 0, d)
            with v.Fori(0, CHUNKS - 1) as c:
                enc_body(c, True)
            enc_body(CHUNKS - 1, False)
            v.wait_ge(S["lat"], 1)
            v.tensor_tensor(zc[:, :].rearrange("p (g b) -> p g b", g=4), p_t[:, 0:32].rearrange("p (g b) -> p g b", g=4),
                            A("bd").rearrange("p (g o) -> p g o", o=1).broadcast_to([128, 4, B]), ALU.add).then_inc(S["zc"], 1)
            v.memset(G[:, 0, 0, :], 0.0).then_inc(S["zc"], 1)
            v.memset(ha[:, :], 0.0).then_inc(S["zc"], 1)
            v.memset(hb[:, :], 0.0).then_inc(S["zc"], 1)
            v.wait_ge(S["zc"], 4)
            v.tensor_copy(zcs[0][:, :], zc[:, :]).then_inc(S["zcs"], 1)
            v.wait_ge(S["zcs"], 1)
            v.tensor_tensor(zcs[1][:, :], zc[:, :], zcs[0][:, :], ALU.subtract).then_inc(S["zcs"], 1)

            def mlp(u, k):
                if u == 1:
                    v.wait_ge(S["f_mm"], k + 1)
                    v.scalar_tensor_tensor(h2[:, :], p_t[0:D, 0:CC], Bc("boA"), h1T[:, bass.ds(k * CC, CC)], ALU.add,
                                           ALU.add).then_inc(S["h2"], 1)
                elif u == 3:
                    v.wait_ge(S["fvar"], k + 1)
                    v.tensor_scalar(var[:, :], p_small[0:D, CC:2 * CC], EPS, None, ALU.add).then_inc(S["varp"], 1)
                    v.tensor_scalar(var_nh[:, :], p_small[0:D, CC:2 * CC], EPS, -0.5, ALU.add, ALU.mult)
                elif u == 4:
                    v.wait_ge(S["varp"], 2 * k + 1)
                    v.tensor_scalar(ru[:, :].bitcast(I32), var[:, :].bitcast(I32), 1, None,
                                    ALU.logical_shift_right).then_inc(S["varp"], 1)
                    v.wait_ge(S["varp"], 2 * k + 2)
                    v.tensor_scalar(rstd[:, :].bitcast(I32), ru[:, :].bitcast(I32), -1.0, ROOT_MAGIC, ALU.mult,
                                    ALU.add).then_inc(S["vseed"], 1)
                elif u == 7:
                    v.wait_ge(S["newton"], 12 * k + 12)
                    v.tensor_tensor(xn[0:D, :], p_small[0:D, 0:CC], rstd[:, :], ALU.mult).then_inc(S["xn"], 1)
                elif u == 8:
                    v.wait_ge(S["xn"], k + 1)
                    v.tensor_tensor(parts[0:D, :], h2[:, :], xn[0:D, :], ALU.add).then_inc(S["at"], 1)
                elif u == 9:
                    v.wait_ge(S["usq"], k + 1)
                    v.tensor_scalar(uin[:, :], usq[:, :], GELU_C, 1.0, ALU.mult, ALU.add).then_inc(S["uin"], 1)
                elif u == 10:
                    v.wait_ge(S["uin"], k + 1)
                    v.tensor_tensor(uin2[:, :], uin[:, :], p_b[:, 0:256], ALU.mult).then_inc(S["uin2"], 1)
                elif u == 12:
                    v.wait_ge(S["uth"], k + 1)
                    v.scalar_tensor_tensor(ug[:, :], uth[:, :], 1.0, p_b[:, 0:256], ALU.add, ALU.mult).then_inc(S["ug"], 1)
                elif u == 13:
                    v.wait_ge(S["y2_mm"], k + 1)
                    v.wait_ge(S["wrow"], k + 1)
                    v.scalar_tensor_tensor(parts[D:128, :], p_x1[D:128, 0:CC], A("b2")[D:128, :],
                                           wrow[D:128, bass.ds(k * CC, CC)], ALU.add, ALU.mult).then_inc(S["bt"], 1)

            def dec_body(k, behind):
                for u in range(CH_T):
                    step(k * CH_T + (T + u), u % 2, B, H[:, 0:B] if u == 0 else hist[:, u * B:u * B + B])
                    if behind:
                        mlp(u, k - 1)
                    if u == 1:
                        v.tensor_copy(hist[:, 0:B], H[:, 0:B]).then_inc(S["first_h"], 1)

            dec_body(0, False)
            with v.Fori(1, CHUNKS) as k:
                dec_body(k, True)
            for u in range(CH_T):
                mlp(u, CHUNKS - 1)

            v.wait_ge(S["wc_mm"], 1)
            v.tensor_copy(wcol[:, :], p_t[0:HALF, 0:16]).then_inc(S["wcol"], 1)
            v.wait_ge(S["wcol"], 1)

            def own(i):
                return wrow[0:HALF, i * HALF * B:(i + 1) * HALF * B].rearrange("p (t b) -> p t b", b=B)

            def rival(j):
                return wcol[:, 8 * j:8 * j + 8].rearrange("p (o b) -> p o b", o=1).broadcast_to([HALF, HALF, B])

            def tb(ap):
                return ap[:, :].rearrange("p (t b) -> p t b", b=B)

            for j in range(2):
                v.tensor_tensor(tb(equal[j]), own(j), rival(j), ALU.is_equal).then_inc(S["equal"], 1)
            for j in range(2):
                for i in range(2):
                    v.tensor_tensor(tb(beats[j][i]), own(i), rival(j), ALU.is_le if j < i else ALU.is_lt
                                    ).then_inc(S["beats"], 1)
            v.wait_ge(S["equal"], 2)
            for j in range(2):
                v.tensor_tensor(tb(tie[j]), tb(equal[j]),
                                A("before", HALF).rearrange("p (t o) -> p t o", o=1).broadcast_to([HALF, HALF, B]),
                                ALU.mult).then_inc(S["beats"], 1)
            v.wait_ge(S["rank"], 1)
            v.tensor_scalar(keep[:, :], p_small[:, 0:CHUNKS], KEEP - 0.5, None, ALU.is_lt).then_inc(S["keep"], 1)
            v.wait_ge(S["keep"], 1)
            abv = ab[:, :].rearrange("p (k s d) -> p k s d", k=CHUNKS, s=2)
            for c in range(4):
                k = slice(3 * c, 3 * c + 3)
                v.tensor_tensor(routed[:, k, :], abv[:, k, 1, :],
                                keep[:, k].rearrange("p (k o) -> p k o", o=1).broadcast_to([128, 3, D]),
                                ALU.mult).then_inc(S["routed"], 1)
            for c in range(4):
                k = slice(3 * c, 3 * c + 3)
                v.wait_ge(S["routed"], c + 1)
                v.tensor_tensor(fin[:, k, :], routed[:, k, :], abv[:, k, 0, :], ALU.add).then_inc(S["fin"], 1)


def kernel(**inputs):
    import numpy as np
    import concourse.bacc as bacc
    from concourse.bass_utils import run_bass_kernel_spmd

    f = np.float32
    inp = {k: np.asarray(v) for k, v in inputs.items()}
    pa, pb = np.zeros((128, PA_N), f), np.zeros((65, PB_N), f)

    def put(name, val):
        val = np.asarray(val, f)
        pa[:val.shape[0], PA[name][0]:PA[name][1]] = val

    def putb(name, val):
        val = np.asarray(val, f)
        pb[:val.shape[0], PB[name][0]:PB[name][1]] = val

    def diagonal(m):
        z = np.zeros((128, 128), f)
        z[:64, :64] = m
        z[64:, 64:] = m
        return z

    def gates(m):
        m = m.reshape(m.shape[0], 4, HID)
        return np.concatenate([m[:, k] for k in (2, 1, 0, 3)], axis=1)

    def twice(v):
        return np.concatenate([v, v])[:, None]

    eye = np.eye(128, dtype=f)
    put("ident", eye)
    put("wq", diagonal(inp["L0_tok_Wq"].T))
    put("wk", diagonal(inp["L0_tok_Wk"]))
    put("wv", diagonal(inp["L0_tok_Wv"].T))
    for e in range(2):
        wo, res = np.zeros((128, D), f), np.zeros((128, D), f)
        wo[64 * e:64 * e + 64] = inp["L0_tok_Wo"].T
        res[64 * e:64 * e + 64] = np.eye(D, dtype=f) / (GS * GS)
        put(f"wo{e}", wo)
        put(f"res{e}", res)
    q, c = np.arange(128)[:, None], np.arange(16)[None]
    put("headmask", (q // 64 == c // 8) & (q % 64 // 8 == c % 8))
    row, pix = np.arange(128)[:, None], np.arange(512)[None]
    put("groupmask", np.where(row // 16 % 2 == pix % 16 // 8, 0.0, NEG))
    put("bq", twice(inp["L0_tok_bq"]))
    put("bv", twice(inp["L0_tok_bv"]))
    for n in "fbd":
        put("U" + n, gates(inp["L0_attn_U" + n]))
    wd = gates(inp["L0_attn_Wd"])
    put("Wd0", wd[:HID])
    put("Wd1", wd[HID:])
    put("bd", gates(inp["L0_attn_bd"][None]).reshape(4, HID).T)
    put("Wo", inp["L0_attn_Wo"])
    put("w2a", np.pad(inp["L0_ffn_w2"][:128], ((0, 0), (D, 0))))
    put("w2b", np.pad(inp["L0_ffn_w2"][128:], ((0, 0), (D, 0))))
    put("before", np.arange(HALF)[:, None] < np.arange(HALF)[None])
    putb("center", np.tile(np.eye(D) - 1.0 / D, 2))
    putb("mean", np.full((D, 128), 1.0 / D))
    putb("bo", inp["L0_tok_bo"][:, None])
    putb("boA", inp["L0_attn_bo"][:, None])
    put("b2", twice(inp["L0_ffn_b2"]))
    for n, b in (("Wf", "bf"), ("Wb", "bb")):
        putb(n, gates(np.concatenate([inp["L0_attn_" + n], inp["L0_attn_" + b][None]])))
    putb("w1", np.concatenate([inp["L0_ffn_w1"], inp["L0_ffn_b1"][None]]))
    putb("wr", np.repeat(np.concatenate([inp["L0_ffn_wr"], inp["L0_ffn_br"][None]]), 128, axis=1))

    arrays = {
        "x": np.ascontiguousarray(inp["x"]),
        "ids": np.ascontiguousarray(inp["x_txt"].T),
        "table": np.ascontiguousarray(inp["L0_txt_shared_embedding"]),
        "hashw": np.ascontiguousarray(inp["L0_txt_hash_weights_table"]),
        "packa": pa, "packb": pb,
    }
    nc = bacc.Bacc("TRN2", target_bir_lowering=False, num_devices=1)
    aps = [nc.dram_tensor(n, a.shape, mybir.dt.from_np(a.dtype), kind="ExternalInput").ap() for n, a in arrays.items()]
    out = nc.dram_tensor("out", (TOK, D), F32, kind="ExternalOutput").ap()
    build(nc, *aps, out)
    r = run_bass_kernel_spmd(nc, [arrays], core_ids=[0])
    got = r.results[0]["out"].reshape(T, B, D)
    return np.ascontiguousarray(got.transpose(1, 0, 2))
```

```python
from contextlib import ExitStack

import concourse.bass as bass
from concourse import mybir

F32 = mybir.dt.float32
F16 = mybir.dt.float16
BF16 = mybir.dt.bfloat16
I32 = mybir.dt.int32
ALU = mybir.AluOpType
ACT = mybir.ActivationFunctionType
AX = mybir.AxisListType

B, D, W = 8, 64, 64
GS, NH = 8, 8
T_IMG, T_TXT = (W // GS) ** 2, 128
T = T_IMG + T_TXT
HID = 128
PAIRS = B // 2
STRIPS = W // GS
SC = GS * B
TOK = T * B
CH_T = 16
CC = CH_T * B
CHUNKS = T // CH_T
IMG_CHUNKS = T_IMG // CH_T
HALF = T // 2
KEEP = max(1, int(0.5 * T)) - 1
EPS = 1e-5

HASH_P, HASH_M, HASH_IC = 100003, 12500, 4
HASH_A = (12345, 20011)
HASH_B = (6789, 54321)
VOCAB = 25000
DIGIT = 128

H_SCALE = 2.0 ** 15
U_SCALE = 2.0 ** 4
SEED_SCALE = 2.0 ** 5
SEED_IDENT = H_SCALE * U_SCALE / SEED_SCALE
Z_ACT = 0.5 / (H_SCALE * U_SCALE)
NEG = -30000.0
ROOT_MAGIC = float(0x5f3759df)
GELU_C, GELU_S = 0.044715, 0.7978845608028654

PA = {}
_at = 0
for _name, _n in (("ident", 128), ("wq", 128), ("wk", 128), ("wv", 128), ("wo0", D), ("wo1", D), ("res0", D), ("res1", D),
                  ("headmask", 16), ("groupmask", 512), ("bq", 1), ("bv", 1),
                  ("Uf", 512), ("Ub", 512), ("Ud", 512), ("Wd0", 512), ("Wd1", 512), ("bd", 4),
                  ("Wo", D), ("w2a", 128), ("w2b", 128), ("b2", 1), ("before", HALF)):
    PA[_name] = (_at, _at + _n)
    _at += _n
PA_N = _at
PA_FIRST = PA["Uf"][0]
PB = {}
_at = 0
for _name, _n in (("center", 128), ("mean", 128), ("bo", 1), ("boA", 1),
                  ("Wf", 512), ("Wb", 512), ("w1", 256), ("wr", 128)):
    PB[_name] = (_at, _at + _n)
    _at += _n
PB_N = _at


def build(nc, x, ids, table, hashw, packa, packb, out):
    with ExitStack() as ctx:
        def sb(name, shape, dt=F32):
            return ctx.enter_context(nc.sbuf_tensor(name, shape, dt))

        def psum(name):
            return ctx.enter_context(nc.psum_tensor(name, [128, 512], F32))

        def sem(name):
            return ctx.enter_context(nc.semaphore(name))

        ca = sb("ca", [128, PA_N])
        cb = sb("cb", [65, PB_N])

        def A(name, rows=128):
            return ca[0:rows, PA[name][0]:PA[name][1]]

        def Bc(name, rows=D):
            return cb[0:rows, PB[name][0]:PB[name][1]]

        X = sb("X", [128, 2, PAIRS * GS * W])
        Xv = [X[:, s, :].rearrange("q (p w h) -> q p w h", p=PAIRS, w=GS) for s in range(2)]
        Xr = sb("Xr", [128, 2, PAIRS, 4, 128])
        qsum = sb("qsum", [128, STRIPS * PAIRS * GS])
        qp = sb("qp", [128, PAIRS * GS])
        qm = sb("qm", [128, PAIRS * GS * 16])
        qk = sb("qk", [128, PAIRS * GS * 16])
        score = sb("score", [128, 512])
        negmax = sb("negmax", [128, 4])
        esum = sb("esum", [128, 4])
        rsum = sb("rsum", [128, 4])
        prob = sb("prob", [128, 512])
        xT = sb("xT", [128, 2, PAIRS * 4 * 128])
        probT = sb("probT", [128, 512])
        yrow = sb("yrow", [128, 512])
        ysb = sb("ysb", [128, 512])
        cmask = sb("cmask", [128, 512])
        ctxv = sb("ctxv", [128, PAIRS * GS])
        ctxb = sb("ctxb", [128, PAIRS * GS])
        h1T = sb("h1T", [D, TOK])

        idx_i = sb("idx_i", [128, B], I32)
        idf = sb("idf", [128, B])
        hp = sb("hp", [128, 2 * B])
        hx = sb("hx", [128, 2 * B])
        hq = sb("hq", [128, 2 * B], I32)
        hm = sb("hm", [128, 2 * B])
        small = sb("small", [128, B])
        hidx = sb("hidx", [128, 2 * B], I32)
        widx = sb("widx", [128, B], I32)
        emb = sb("emb", [128, 2, B, D])
        hwt = sb("hwt", [128, B, 2])
        txt = sb("txt", [128, B, D])

        sqT = sb("sqT", [D, T_IMG * B])
        spread = sb("spread", [D, T_IMG * B])
        vcol, vhalf, rcol, rtmp = [sb(n, [128, IMG_CHUNKS]) for n in ("vcol", "vhalf", "rcol", "rtmp")]
        txtn = sb("txtn", [128, B, D])
        txt_sq = sb("txt_sq", [128, B, D])
        tmean, tvar, tv_nh, troot, tr1, tr2, t_three = [sb(n, [128, B]) for n in (
            "tmean", "tvar", "tv_nh", "troot", "tr1", "tr2", "t_three")]
        xnT = sb("xnT", [65, TOK])
        seeds = [sb(f"seeds{p}", [128, 2 * CH_T * 32], F16) for p in range(2)]

        ident16 = sb("ident16", [128, 128], F16)
        Ua = sb("Ua", [128, 3 * 512], F16)
        Ul = sb("Ul", [128, 3 * 512], F16)
        Wda = sb("Wda", [128, 2 * 512], F16)
        Wdl = sb("Wdl", [128, 2 * 512], F16)
        G = sb("G", [128, 2, 5, 16])
        prod = sb("prod", [128, 2, 16])
        osc = sb("osc", [128, 16])
        tc = sb("tc", [128, 16])
        H = sb("H", [128, 16])
        ha = sb("ha", [128, 16], F16)
        hb = sb("hb", [128, 16], F16)
        zc = sb("zc", [128, 32])
        zcs = [sb(f"zcs{p}", [128, 32], F16) for p in range(2)]
        hist = sb("hist", [128, CC])
        sq = sb("sq", [D, CC])
        cen = sb("cen", [D, CC])
        var, var_nh, rstd, rt, ru, three_half = [sb(n, [128, 1]) for n in ("var", "var_nh", "rstd", "rt", "ru", "three_half")]
        xn = sb("xn", [65, CC])

        h2 = sb("h2", [D, CC])
        wrow = sb("wrow", [128, TOK])
        usq = sb("usq", [128, 256])
        uin = sb("uin", [128, 256])
        uin2 = sb("uin2", [128, 256])
        uth = sb("uth", [128, 256])
        ug = sb("ug", [128, 256])
        parts = sb("parts", [128, CC])
        ab = sb("ab", [128, CHUNKS * 128])
        wcol = sb("wcol", [HALF, 2 * B])
        beats = [[sb(f"beats{j}{i}", [HALF, HALF * B], BF16) for i in range(2)] for j in range(2)]
        equal = [sb(f"equal{j}", [HALF, HALF * B], BF16) for j in range(2)]
        tie = [sb(f"tie{j}", [HALF, HALF * B], BF16) for j in range(2)]
        ones16 = sb("ones16", [HALF, 2], BF16)
        keep = sb("keep", [128, CHUNKS])
        fin = sb("fin", [128, CHUNKS, D])

        zA, zB, p_small, p_a, p_b, p_x0, p_x1, p_t = [psum(n) for n in (
            "zA", "zB", "p_small", "p_a", "p_b", "p_x0", "p_x1", "p_t")]
        p_x = [p_x0, p_x1]

        s_ca, s_cl, s_cb, s_ids = sem("s_ca"), sem("s_cl"), sem("s_cb"), sem("s_ids")
        s_x = [sem("s_x0"), sem("s_x1")]
        xt_copied = [sem("xt_copied0"), sem("xt_copied1")]
        proj = [sem("proj_f"), sem("proj_b")]
        S = {n: sem("s_" + n) for n in (
            "xr qsum qp_mm qp qm qk_mm qk score_mm score negmax exp rsum xt_mm pt_mm pt y_mm yrow yt_mm y c_mm cmask ctxv ctxb "
            "o_mm h1 wq cen sq var root bc_mm xnT seed_a seed_b hash hidx gath txt tt_mm tt_copy weights memset "
            "tsum tmean tcen tsq tvar tseed tnewton txtn tn_mm tn_copy spread "
            "zgfi zgfi_back zo gates ogate prod cell osc tanhc ha hfull hb wd lat zc zcs "
            "f_mm h2 fcen fsq cenc fvar varp vseed newton fbc xn "
            "r_mm wrow u_mm usq uin uin2 uth ug y2_mm bt at ab_mm ab wc_mm wcol equal beats pool_beats rank keep fin out"
        ).split()}

        block = ctx.enter_context(nc.Block())
        x_dram = x.rearrange("(p two) c (g w) h -> g (two c) p (w h)", two=2, w=GS)

        WEIGHTS = 18
        ROOTS = 13
        EARLY = IMG_CHUNKS - 1

        xt_bank, XT_ORDER = (p_x0, p_x1, p_a, zA), (2, 0, 1, 3)

        tncols = xnT[0:D, T_IMG * B:TOK].rearrange("d (t b) -> d b t", b=B)
        tcols = h1T[:, T_IMG * B:TOK].rearrange("d (t b) -> d b t", b=B)

        z_bank = (zA, p_a)

        def seed_at(d, u):
            return (d * CH_T + (u if d == 0 else CH_T - 1 - u)) * 32

        def half_tokens(h, d):
            return (h if d == 0 else 1 - h) * CH_T // 2

        def seed_half(part, h, d):
            at_ = (d * CH_T + half_tokens(h, d)) * 32
            return seeds[part][:, at_:at_ + CH_T // 2 * 32].rearrange("p (t g b) -> p g t b", g=4, b=B)

        def proj_half(h, d):
            t0 = half_tokens(h, d)
            return p_x[d][:, :].rearrange("p (g t b) -> p g t b", g=4, b=B)[:, :, t0:t0 + CH_T // 2, :]

        def own(i):
            return wrow[0:HALF, i * HALF * B:(i + 1) * HALF * B].rearrange("p (t b) -> p t b", b=B)

        def rival(j, n):
            return wcol[:, 8 * j:8 * j + 8].rearrange("p (o b) -> p o b", o=1).broadcast_to([HALF, n, B])

        def tb(ap):
            return ap[:, :].rearrange("p (t b) -> p t b", b=B)

        def earlier(lo, hi):
            return A("before", HALF)[:, lo:hi].rearrange("p (t o) -> p t o", o=1).broadcast_to([HALF, hi - lo, B])

        STORE_CHUNKS = 3
        BEATS = 7

        def store(queue, c):
            k0, k1 = STORE_CHUNKS * c, STORE_CHUNKS * (c + 1)
            queue.wait_ge(S["fin"], k1)
            queue.dma_start(out[k0 * CC:k1 * CC, :].rearrange("(k p) d -> p k d", p=128),
                            fin[:, k0:k1, :]).then_inc(S["out"], 16)

        @block.sync
        def _(sp):
            def load_strip(n, s):
                sp.dma_start(X[:, s, :].rearrange("q (p n) -> q p n", p=PAIRS),
                             x_dram[bass.ds(n, 1)].rearrange("g q p n -> (g q) p n")).then_inc(s_x[s], 16)
            sp.dma_start(idx_i[:, :], ids).then_inc(s_ids, 16)
            load_strip(0, 0)
            sp.dma_start(ca[:, 0:PA_FIRST], packa[:, 0:PA_FIRST]).then_inc(s_ca, 16)
            sp.dma_start(cb[:, :], packb).then_inc(s_cb, 16)
            load_strip(1, 1)
            sp.dma_start(ca[:, PA_FIRST:PA_N], packa[:, PA_FIRST:PA_N]).then_inc(s_cl, 16)
            with sp.Fori(1, STRIPS // 2) as i:
                for s in range(2):
                    sp.wait_ge(S["qsum"], 2 * i + s - 1)
                    sp.wait_ge(S["xr"], 2 * i + s - 1)
                    load_strip(2 * i + s, s)
            store(sp, 0)
            store(sp, 2)
            sp.wait_ge(S["out"], 16 * CHUNKS // STORE_CHUNKS)

        @block.gpsimd
        def _(pool):
            pool.memset(G[:, :, 0:4, :], 0.0).then_inc(S["gates"], 1)
            pool.memset(G[:, :, 4, :], 0.0).then_inc(S["ogate"], 1)
            pool.memset(ha[:, :], 0.0).then_inc(S["ha"], 1)
            pool.memset(hb[:, :], 0.0).then_inc(S["hb"], 1)
            pool.memset(three_half[:, :], 1.5).then_inc(S["memset"], 1)
            pool.memset(t_three[:, :], 1.5).then_inc(S["memset"], 1)
            pool.memset(ones16[:, :], 1.0).then_inc(S["memset"], 1)
            pool.wait_ge(S["memset"], 3)
            pool.memset(xn[64:65, :], 1.0).then_inc(S["memset"], 1)
            pool.memset(xnT[64:65, :], 1.0).then_inc(S["memset"], 1)
            pool.wait_ge(S["memset"], 5)

            done = [0]

            def h_(ins):
                done[0] += 1
                ins.then_inc(S["hash"], 1)
                pool.wait_ge(S["hash"], done[0])

            def mod(val, m):
                h_(pool.tensor_scalar(hq[:, :], val, 1.0 / m, None, ALU.mult))
                h_(pool.tensor_scalar(hm[:, :], hq[:, :], -float(m), None, ALU.mult))
                h_(pool.tensor_tensor(val, val, hm[:, :], ALU.add))
                h_(pool.tensor_scalar(hm[:, :], val, 0.0, float(m), ALU.is_lt, ALU.mult))
                h_(pool.tensor_tensor(val, val, hm[:, :], ALU.add))
                h_(pool.tensor_scalar(hm[:, :], val, float(m), -float(m), ALU.is_ge, ALU.mult))
                h_(pool.tensor_tensor(val, val, hm[:, :], ALU.add))

            pool.wait_ge(s_ids, 16)
            h_(pool.tensor_copy(idf[:, :], idx_i[:, :]))
            for k in range(2):
                h_(pool.tensor_scalar(hp[:, k * B:k * B + B], idf[:, :], float(HASH_A[k] // DIGIT), None, ALU.mult))
                h_(pool.tensor_scalar(hx[:, k * B:k * B + B], idf[:, :], float(HASH_A[k] % DIGIT), float(HASH_B[k]),
                                   ALU.mult, ALU.add))
            mod(hp[:, :], HASH_P)
            h_(pool.tensor_scalar(hp[:, :], hp[:, :], float(DIGIT), None, ALU.mult))
            mod(hp[:, :], HASH_P)
            h_(pool.tensor_tensor(hp[:, :], hp[:, :], hx[:, :], ALU.add))
            mod(hp[:, :], HASH_P)
            mod(hp[:, :], HASH_M)
            h_(pool.tensor_scalar(small[:, :], idf[:, :], float(HASH_IC), None, ALU.is_lt))
            h_(pool.tensor_scalar(hp[:, :], hp[:, :], float(HASH_IC), None, ALU.add))
            for k in range(2):
                c = slice(k * B, k * B + B)
                h_(pool.tensor_tensor(hx[:, c], hp[:, c], idf[:, :], ALU.subtract))
                h_(pool.tensor_tensor(hx[:, c], hx[:, c], small[:, :], ALU.mult))
            h_(pool.tensor_tensor(hp[:, :], hp[:, :], hx[:, :], ALU.subtract))
            pool.tensor_copy(hidx[:, :], hp[:, :]).then_inc(S["hidx"], 1)
            pool.tensor_scalar(widx[:, :], idf[:, :], float(VOCAB - 1), None, ALU.min).then_inc(S["hidx"], 1)

            pool.wait_ge(S["hidx"], 2)
            for b in range(B):
                for k in range(2):
                    pool.indirect_dma_start(
                        out=emb[:, k, b, :], out_offset=None, in_=table,
                        in_offset=bass.IndirectOffsetOnAxis(ap=hidx[:, k * B + b:k * B + b + 1], axis=0)
                    ).then_inc(S["gath"], 16)
                pool.indirect_dma_start(
                    out=hwt[:, b, :], out_offset=None, in_=hashw,
                    in_offset=bass.IndirectOffsetOnAxis(ap=widx[:, b:b + 1], axis=0)
                ).then_inc(S["gath"], 16)

            wd = [0]

            def w_(ins):
                wd[0] += 1
                ins.then_inc(S["weights"], 1)

            def settle():
                pool.wait_ge(S["weights"], wd[0])

            def g_block(ap, n):
                return ap.rearrange("p (n c) -> p n c", n=n)[:, :, 0:128]

            pool.wait_ge(s_cl, 16)
            pool.wait_ge(s_cb, 16)
            pool.wait_ge(s_ca, 16)
            Uall = ca[:, PA["Uf"][0]:PA["Ud"][1]]
            Wdall = ca[:, PA["Wd0"][0]:PA["Wd1"][1]]
            Win = cb[:, PB["Wf"][0]:PB["Wb"][1]]
            w2all = ca[:, PA["w2a"][0]:PA["w2b"][1]]
            w_(pool.tensor_scalar(Win, Win, SEED_SCALE, None, ALU.mult))
            w_(pool.tensor_scalar(Uall, Uall, U_SCALE, None, ALU.mult))
            w_(pool.tensor_scalar(Wdall, Wdall, U_SCALE, None, ALU.mult))
            w_(pool.tensor_scalar(A("bd"), A("bd"), SEED_SCALE, None, ALU.mult))
            w_(pool.tensor_scalar(A("Wo"), A("Wo"), 1.0 / H_SCALE, None, ALU.mult))
            w_(pool.tensor_scalar(w2all, w2all, 0.5, None, ALU.mult))
            w_(pool.tensor_scalar(ident16[:, :], A("ident"), SEED_IDENT, None, ALU.mult))
            settle()
            w_(pool.tensor_scalar(g_block(Win, 2), g_block(Win, 2), 2.0, None, ALU.mult))
            w_(pool.tensor_scalar(g_block(Uall, 3), g_block(Uall, 3), 2.0, None, ALU.mult))
            w_(pool.tensor_scalar(g_block(Wdall, 2), g_block(Wdall, 2), 2.0, None, ALU.mult))
            w_(pool.tensor_scalar(A("bd")[:, 0:1], A("bd")[:, 0:1], 2.0, None, ALU.mult))
            settle()
            for m in range(3):
                w_(pool.tensor_copy(Ua[:, m * 512:m * 512 + 512], Uall[:, m * 512:m * 512 + 512]))
            settle()
            for m in range(3):
                c = slice(m * 512, m * 512 + 512)
                w_(pool.tensor_tensor(Ul[:, c], Uall[:, c], Ua[:, c], ALU.subtract))
            w_(pool.tensor_copy(zcs[0][:, 0:2], A("bd")[:, 0:2]))
            assert wd[0] == WEIGHTS

            pool.wait_ge(S["gath"], 24 * 16)
            for k in range(2):
                pool.tensor_tensor(emb[:, k, :, :], emb[:, k, :, :],
                                   hwt[:, :, k:k + 1].broadcast_to([128, B, D]), ALU.mult).then_inc(S["txt"], 1)
            pool.wait_ge(S["txt"], 2)
            pool.tensor_tensor(txt[:, :, :], emb[:, 0, :, :], emb[:, 1, :, :], ALU.add).then_inc(S["txt"], 1)

            def each(ap):
                return ap[:, :].rearrange("p (b o) -> p b o", o=1).broadcast_to([128, B, D])

            pool.wait_ge(S["tsum"], 1)
            pool.tensor_scalar(tmean[:, :], tmean[:, :], 1.0 / D, None, ALU.mult).then_inc(S["tmean"], 1)
            pool.wait_ge(S["tmean"], 1)
            pool.tensor_tensor(txtn[:, :, :], txt[:, :, :], each(tmean), ALU.subtract).then_inc(S["tcen"], 1)
            pool.wait_ge(S["tcen"], 1)
            pool.tensor_tensor(txt_sq[:, :, :], txtn[:, :, :], txtn[:, :, :], ALU.mult).then_inc(S["tsq"], 1)
            pool.wait_ge(S["tseed"], 1)
            for r in range(3):
                for m, (o, a, b, op) in enumerate(((tr1, troot, troot, ALU.mult), (tr2, tr1, tv_nh, ALU.mult),
                                                   (tr1, tr2, t_three, ALU.add), (troot, tr1, troot, ALU.mult))):
                    pool.tensor_tensor(o[:, :], a[:, :], b[:, :], op).then_inc(S["tnewton"], 1)
                    pool.wait_ge(S["tnewton"], 4 * r + m + 1)
            pool.tensor_tensor(txtn[:, :, :], txtn[:, :, :], each(troot), ALU.mult).then_inc(S["txtn"], 1)

            pool.tensor_copy(Wda[:, :], Wdall).then_inc(S["wd"], 1)
            pool.wait_ge(S["wd"], 1)
            pool.tensor_tensor(Wdl[:, :], Wdall, Wda[:, :], ALU.subtract).then_inc(S["wd"], 1)

            def newton(k):
                pool.wait_ge(S["vseed"], k + 1)
                for r in range(3):
                    for m, (o, a, b, op) in enumerate(((rt, rstd, rstd, ALU.mult), (ru, rt, var_nh, ALU.mult),
                                                       (rt, ru, three_half, ALU.add), (rstd, rt, rstd, ALU.mult))):
                        if 4 * r + m > 0:
                            pool.wait_ge(S["newton"], k * 12 + (4 * r + m))
                        pool.tensor_tensor(o[:, :], a[:, :], b[:, :], op).then_inc(S["newton"], 1)

            with pool.Fori(0, CHUNKS) as k:
                newton(k)
            pool.wait_ge(S["equal"], 3)
            pool.tensor_tensor(tb(tie[1]), tb(equal[1]), earlier(0, HALF), ALU.mult).then_inc(S["pool_beats"], 1)

        @block.tensor
        def _(pe):
            def mm(o, l, r, start=True, stop=True):
                return pe.matmul(o, l, r, start=start, stop=stop, skip_group_check=True)

            def project(c, d, gates, ahead=False):
                cols = c * CC if d == 0 else (CHUNKS - 1) * CC - c * CC
                for g in gates:
                    last = mm(p_x[d][:, g * CC:g * CC + CC], Bc("Wf" if d == 0 else "Wb", 65)[:, g * 128:g * 128 + 128],
                              xnT[:, bass.ds(cols, CC)])
                if gates[-1] == 3:
                    last.then_inc(proj[d], 1)

            def pixels_out(m, s, e, first=False):
                if e == 0:
                    pe.wait_ge(S["xr"], m + 1)
                if not first:
                    pe.wait_ge(xt_copied[e], (3 - 2 * e) * m)
                for r in XT_ORDER[3 * e:3 + e]:
                    for j in range(4):
                        last = pe.transpose(xt_bank[r][:, j * 128:j * 128 + 128], Xr[:, s, r, j, :], A("ident"))
                    last.then_inc(S["xt_mm"], 1)

            def query(m):
                pe.wait_ge(S["qsum"], m + 1)
                mm(p_small[:, 0:32], A("wq"), qsum[:, bass.ds(m * 32, 32)]).then_inc(S["qp_mm"], 1)

            def query_key(m):
                pe.wait_ge(S["qm"], m + 1)
                pe.wait_ge(xt_copied[0], 3 * m + 1)
                mm(p_a[:, :], A("wk"), qm[:, :]).then_inc(S["qk_mm"], 1)

            def scores(m, s):
                pe.wait_ge(S["qk"], m + 1)
                for p in range(PAIRS):
                    for j in range(4):
                        c = (p * GS + 2 * j) * 16
                        last = mm(p_b[32 * p:32 * p + 32, j * 128:j * 128 + 128], qk[:, c:c + 32], Xr[:, s, p, j, :])
                last.then_inc(S["score_mm"], 1)

            def probs_out(n):
                pe.wait_ge(S["exp"], n + 1)
                for j in range(4):
                    last = pe.transpose(p_t[:, j * 128:j * 128 + 128], prob[:, j * 128:j * 128 + 128], A("ident"))
                last.then_inc(S["pt_mm"], 1)

            def pixel_sums(n, s, next_copied):
                pe.wait_ge(S["pt"], n + 1)
                if next_copied is not None:
                    pe.wait_ge(xt_copied[1], next_copied)
                for p in range(PAIRS):
                    for j in range(4):
                        c = (p * 4 + j) * 128
                        last = mm(zA[32 * p:32 * p + 32, j * 128:j * 128 + 128],
                                  probT[:, j * 128 + 32 * p:j * 128 + 32 * p + 32], xT[:, s, c:c + 128])
                last.then_inc(S["y_mm"], 1)

            def sums_out(n):
                pe.wait_ge(S["yrow"], n + 1)
                for j in range(4):
                    last = pe.transpose(p_t[:, j * 128:j * 128 + 128], yrow[:, j * 128:j * 128 + 128], A("ident"))
                last.then_inc(S["yt_mm"], 1)

            def context(n):
                pe.wait_ge(S["y"], n + 1)
                mm(zB[:, :], A("wv"), ysb[:, :]).then_inc(S["c_mm"], 1)

            def attn_out(n, o=zB):
                pe.wait_ge(S["ctxb"], n + 1)
                for e in range(2):
                    mm(o[0:D, 32 * e:32 * e + 32], A(f"wo{e}"), ctxb[:, :], start=(e == 0), stop=False)
                    last = mm(o[0:D, 32 * e:32 * e + 32], A(f"res{e}"), qsum[:, bass.ds(n * 32, 32)], start=False)
                last.then_inc(S["o_mm"], 1)

            def strips(n, u, first):
                query(n + 1)
                if not first:
                    sums_out(n - 1)
                pixels_out(n + 1, 1 - u, 0)
                if not first:
                    context(n - 1)
                pixels_out(n + 1, 1 - u, 1)
                query_key(n + 1)
                probs_out(n)
                if not first:
                    attn_out(n - 1)
                pixel_sums(n, u, n + 2)
                scores(n + 1, 1 - u)

            pe.wait_ge(s_ca, 16)
            pe.wait_ge(S["wq"], 1)
            pixels_out(0, 0, 0, True)
            pixels_out(0, 0, 1, True)
            query(0)
            query_key(0)
            scores(0, 0)
            strips(0, 0, True)
            with pe.Fori(0, STRIPS // 2 - 1) as i:
                for u in range(2):
                    strips(2 * i + (u + 1), 1 - u, False)
            sums_out(STRIPS - 2)
            pe.wait_ge(S["h1"], STRIPS - 2)
            context(STRIPS - 2)
            pe.wait_ge(xt_copied[0], 3 * STRIPS)
            pe.wait_ge(xt_copied[1], STRIPS)
            pe.wait_ge(S["txt"], 3)
            for b in range(B):
                last = pe.transpose(p_x[b // 4][0:D, (b % 4) * 128:(b % 4) * 128 + 128], txt[:, b, :], A("ident"))
            last.then_inc(S["tt_mm"], 1)
            def centre(c0, c1):
                mm(p_b[:, c0 * CC:c1 * CC], Bc("center"), h1T[:, c0 * CC:c1 * CC]).then_inc(S["cen"], 1)

            def variances(c0, c1):
                for k in range(c0, c1):
                    last = mm(p_small[:, k:k + 1], sqT[:, k * CC:k * CC + CC], Bc("mean")[:, 0:1])
                last.then_inc(S["var"], 1)

            def spread_roots(c0, c1):
                for k in range(c0, c1):
                    last = mm(p_t[:, k * CC:k * CC + CC], rcol[:, k:k + 1].broadcast_to([128, 128]), A("ident"))
                last.then_inc(S["bc_mm"], 1)

            probs_out(STRIPS - 1)
            pe.wait_ge(s_cb, 16)
            pe.wait_ge(S["h1"], 2 * EARLY)
            centre(0, EARLY)
            attn_out(STRIPS - 2)
            pixel_sums(STRIPS - 1, 1, None)
            pe.wait_ge(S["sq"], 1)
            variances(0, EARLY)
            sums_out(STRIPS - 1)
            pe.wait_ge(S["h1"], STRIPS - 1)
            context(STRIPS - 1)
            pe.wait_ge(S["txtn"], 1)
            pe.wait_ge(S["tt_copy"], 2)
            for b in range(B):
                last = pe.transpose(p_x[b // 4][0:D, (b % 4) * 128:(b % 4) * 128 + 128], txtn[:, b, :], A("ident"))
            last.then_inc(S["tn_mm"], 1)
            pe.wait_ge(S["root"], ROOTS)
            spread_roots(0, EARLY)
            pe.wait_ge(S["weights"], WEIGHTS)
            pe.wait_ge(S["memset"], 5)
            pe.wait_ge(S["tn_copy"], 2)
            project(0, 1, range(4))
            pe.wait_ge(S["xnT"], 1)
            project(0, 0, range(4))

            def last_chunk(u):
                if u == 1:
                    attn_out(STRIPS - 1, p_small)
                elif u == 3:
                    pe.wait_ge(S["h1"], STRIPS)
                    centre(EARLY, IMG_CHUNKS)
                elif u == 5:
                    pe.wait_ge(S["sq"], 2)
                    variances(EARLY, IMG_CHUNKS)
                elif u == 13:
                    pe.wait_ge(S["root"], 2 * ROOTS)
                    spread_roots(EARLY, IMG_CHUNKS)

            def U(part, net, g):
                return part[:, net * 512 + g * 128:net * 512 + g * 128 + 128]

            def z_gfi(d):
                return z_bank[d][:, 0:3 * B].rearrange("p (g b) -> p g b", g=3)

            def z_o(d):
                return zB[:, 8 * d:8 * d + 8]

            def seed(rows, dirs, t):
                pe.wait_ge(S["gates"], t + 1)
                for part in range(2):
                    for d in range(dirs):
                        mm(z_gfi(d), ident16[:, :], rows(part, d)[:, 0:24], start=(part == 0))
                pe.wait_ge(S["ogate"], t + 1)
                for part in range(2):
                    for d in range(dirs):
                        mm(z_o(d), ident16[:, :], rows(part, d)[:, 24:32], start=(part == 0 and d == 0))

            def recur(nets, t):
                z = lambda g, d: z_o(d) if g == 3 else z_gfi(d)[:, g, :]

                def high(gs):
                    for d, net in enumerate(nets):
                        for g in gs:
                            for part in (Ua, Ul):
                                mm(z(g, d), U(part, net, g), ha[:, 8 * d:8 * d + 8], start=False)

                def low(gs, d):
                    for g in gs:
                        last = mm(z(g, d), U(Ua, nets[d], g), hb[:, 8 * d:8 * d + 8], start=False)
                    return last

                pe.wait_ge(S["ha"], t + 1)
                high(range(3))
                if len(nets) == 1:
                    high([3])
                pe.wait_ge(S["hb"], t + 1)
                low(range(3), 0).then_inc(S["zgfi"], 1)
                if len(nets) == 2:
                    low(range(3), 1).then_inc(S["zgfi_back"], 1)
                    high([3])
                    low([3], 0)
                low([3], len(nets) - 1).then_inc(S["zo"], 1)

            def enc_body(c, ahead, extra=None):
                for u in range(CH_T):
                    if u % 8 == 0:
                        pe.wait_ge(S["seed_b"], 4 * c + (2 + u // 4))
                    seed(lambda part, d: seeds[part][:, seed_at(d, u):seed_at(d, u) + 32], 2, c * CH_T + u)
                    if ahead and 4 <= u < 12:
                        if u == 4:
                            pe.wait_ge(S["seed_b"], 4 * c + 3)
                        project(c + 1, (u - 4) // 4, [u % 4])
                    if extra is not None:
                        extra(u)
                    recur((0, 1), c * CH_T + u)

            enc_body(0, True, last_chunk)
            pe.wait_ge(S["xnT"], 2)
            with pe.Fori(1, CHUNKS - 1) as c:
                enc_body(c, True)
            enc_body(CHUNKS - 1, False)

            pe.wait_ge(S["hb"], T + 1)
            pe.wait_ge(S["wd"], 2)
            for g in range(4):
                for d in range(2):
                    c, b = slice(d * 512 + g * 128, d * 512 + g * 128 + 128), slice(8 * d, 8 * d + 8)
                    for part, state in ((Wda, ha), (Wdl, ha), (Wda, hb)):
                        last = mm(p_t[:, 8 * g:8 * g + 8], part[:, c], state[:, b],
                                  start=(g == 0 and d == 0 and part is Wda and state is ha))
            last.then_inc(S["lat"], 1)
            pe.wait_ge(S["zcs"], 2)

            def mlp(u, k):
                if u == 1:
                    mm(p_t[0:D, 0:CC], A("Wo"), hist[:, :]).then_inc(S["f_mm"], 1)
                elif u == 2:
                    pe.wait_ge(S["h2"], k + 1)
                    mm(p_small[:, 0:CC], Bc("center"), h2[:, :]).then_inc(S["fcen"], 1)
                elif u == 3:
                    pe.wait_ge(S["fsq"], k + 1)
                    mm(p_a[:, 0:1], sq[:, :], Bc("mean")[:, 0:1]).then_inc(S["fvar"], 1)
                elif u == 6:
                    pe.wait_ge(S["newton"], 12 * k + 12)
                    mm(p_a[:, CC:2 * CC], rstd[:, :].broadcast_to([128, 128]), A("ident")).then_inc(S["fbc"], 1)
                elif u in (7, 8):
                    h = u - 7
                    pe.wait_ge(S["xn"], k + 1)
                    mm(p_b[:, h * 128:h * 128 + 128], Bc("w1", 65)[:, h * 128:h * 128 + 128], xn[:, :]).then_inc(S["u_mm"], 1)
                elif u == 9:
                    mm(p_a[:, 256:256 + CC], Bc("wr", 65), xn[:, :]).then_inc(S["r_mm"], 1)
                elif u == 11:
                    pe.wait_ge(S["ug"], k + 1)
                    mm(p_x1[:, 0:CC], A("w2a"), ug[:, 0:128], stop=False)
                elif u == 12:
                    mm(p_x1[:, 0:CC], A("w2b"), ug[:, 128:256], start=False).then_inc(S["y2_mm"], 1)
                elif u == 13:
                    pe.wait_ge(S["bt"], k + 1)
                    pe.wait_ge(S["at"], k + 1)
                    pe.transpose(p_x0[:, 0:CC], parts[:, :], A("ident")).then_inc(S["ab_mm"], 1)

            def dec_body(k, behind, extra={}):
                for u in range(CH_T):
                    seed(lambda part, d: zcs[part][:, :], 1, k * CH_T + (T + u))
                    if behind:
                        mlp(u, k - 1)
                    if u in extra:
                        extra[u]()
                    recur((2,), k * CH_T + (T + u))

            rivals = wrow[0:1, :].rearrange("p (h t b) -> p h t b", h=2, b=B)

            def rival_weights(hf):
                pe.wait_ge(S["wrow"], CHUNKS // 2 * (hf + 1))
                for b in range(B):
                    last = pe.transpose(p_t[0:HALF, 256 + 8 * hf + b:256 + 8 * hf + b + 1], rivals[:, hf, :, b],
                                        A("ident", 1)[:, 0:1])
                last.then_inc(S["wc_mm"], 1)

            dec_body(0, False)
            with pe.Fori(1, CHUNKS - 1) as k:
                dec_body(k, True)
            dec_body(CHUNKS - 1, True, {4: lambda: rival_weights(0)})
            pe.wait_ge(S["hb"], 2 * T + 1)
            for u in range(CH_T):
                mlp(u, CHUNKS - 1)
                if u == 10:
                    rival_weights(1)
            pe.wait_ge(S["ab"], CHUNKS)

            pe.wait_ge(S["beats"], BEATS)
            pe.wait_ge(S["pool_beats"], 1)
            for k in range(CHUNKS):
                ih, c = k // (CHUNKS // 2), (k % (CHUNKS // 2)) * CC
                for m, part in enumerate((beats[0][ih], beats[1][ih], tie[ih])):
                    last = mm(p_small[:, k:k + 1], part[:, c:c + CC], ones16[:, 0:1], start=(k == 0 and m == 0))
            last.then_inc(S["rank"], 1)

        @block.scalar
        def _(act):
            def regroup(m, s, loads):
                act.wait_ge(s_x[s], 16 * loads)
                for p in range(PAIRS):
                    last = act.copy(Xr[:, s, p, :, :].rearrange("q j (w c) -> q j w c", c=16),
                                    Xv[s][:, p, :, :].rearrange("q w (j c) -> q j w c", c=16))
                last.then_inc(S["xr"], 1)

            def pixels(m, s, r):
                act.wait_ge(S["xt_mm"], 4 * m + (XT_ORDER.index(r) + 1))
                act.copy(xT[:, s, r * 512:r * 512 + 512], xt_bank[r][:, :]).then_inc(xt_copied[0], 1)

            def query_key(m):
                act.wait_ge(S["qk_mm"], m + 1)
                act.copy(qk[:, :], p_a[:, :]).then_inc(S["qk"], 1)

            def exps(m):
                act.wait_ge(S["negmax"], m + 1)
                for j in range(4):
                    c = j * 128
                    last = act.activation(prob[:, c:c + 128], score[:, c:c + 128], ACT.Exp, bias=negmax[:, j:j + 1],
                                          accum_out=esum[:, j:j + 1])
                last.then_inc(S["exp"], 1)

            def probs(n):
                act.wait_ge(S["pt_mm"], n + 1)
                act.copy(probT[:, :], p_t[:, :]).then_inc(S["pt"], 1)

            def sums(n):
                act.wait_ge(S["y_mm"], n + 1)
                act.wait_ge(S["rsum"], n + 1)
                for j in range(4):
                    last = act.activation(yrow[:, j * 128:j * 128 + 128], zA[:, j * 128:j * 128 + 128], ACT.Copy,
                                          scale=rsum[:, j:j + 1])
                last.then_inc(S["yrow"], 1)

            def sums_by_token(n):
                act.wait_ge(S["yt_mm"], n + 1)
                act.copy(ysb[:, :].rearrange("q (p j c) -> q j p c", p=PAIRS, j=4),
                         p_t[:, :].rearrange("q (j p c) -> q j p c", p=PAIRS, j=4)).then_inc(S["y"], 1)

            def strips(n, u, loads, last):
                pixels(n + 1, 1 - u, 0)
                pixels(n + 1, 1 - u, 1)
                probs(n)
                query_key(n + 1)
                if not last:
                    regroup(n + 2, u, loads)
                sums(n)
                sums_by_token(n)
                if not last:
                    pixels(n + 2, u, 2)
                exps(n + 1)

            regroup(0, 0, 1)
            pixels(0, 0, 2)
            query_key(0)
            pixels(0, 0, 0)
            pixels(0, 0, 1)
            regroup(1, 1, 1)
            pixels(1, 1, 2)
            exps(0)
            with act.Fori(0, STRIPS // 2 - 1) as i:
                for u in range(2):
                    strips(2 * i + u, u, i + 2, False)
            strips(STRIPS - 2, 0, 0, True)
            def squares(q, c0, c1):
                act.wait_ge(S["cen"], q)
                act.activation(sqT[:, c0 * CC:c1 * CC], p_b[0:D, c0 * CC:c1 * CC], ACT.Square).then_inc(S["sq"], 1)

            def roots(q, c0, c1):
                act.wait_ge(S["bc_mm"], q)
                act.copy(spread[:, c0 * CC:c1 * CC], p_t[0:D, c0 * CC:c1 * CC]).then_inc(S["spread"], 1)

            probs(STRIPS - 1)
            squares(1, 0, EARLY)
            act.wait_ge(S["tt_mm"], 1)
            act.copy(tcols[:, 4:8, :], p_x1[0:D, :].rearrange("d (b t) -> d b t", b=4)).then_inc(S["tt_copy"], 1)
            sums(STRIPS - 1)
            sums_by_token(STRIPS - 1)
            act.wait_ge(S["tn_mm"], 1)
            act.copy(tncols[:, 4:8, :], p_x1[0:D, :].rearrange("d (b t) -> d b t", b=4)).then_inc(S["tn_copy"], 1)
            roots(1, 0, EARLY)

            def last_chunk(u):
                if u == 3:
                    squares(2, EARLY, IMG_CHUNKS)
                elif u == 13:
                    roots(2, EARLY, IMG_CHUNKS)

            def seeds_high(c, h, d):
                act.wait_ge(proj[d], c + 1)
                act.copy(seed_half(0, h, d), proj_half(h, d)).then_inc(S["seed_a"], 1)

            def step(t, par, nb):
                def gates(d):
                    return act.activation(G[:, par, 1:4, B * d:B * d + B],
                                          z_bank[d][:, 0:3 * B].rearrange("p (g b) -> p g b", g=3), ACT.Tanh, scale=Z_ACT)
                act.wait_ge(S["zgfi"], t + 1)
                last = gates(0)
                if nb == 2 * B:
                    act.wait_ge(S["zgfi_back"], t + 1)
                    last = gates(1)
                last.then_inc(S["gates"], 1)
                act.wait_ge(S["zo"], t + 1)
                act.activation(G[:, par, 4, 0:nb], zB[:, 0:nb], ACT.Tanh, scale=Z_ACT).then_inc(S["ogate"], 1)
                act.wait_ge(S["cell"], t + 1)
                act.activation(tc[:, 0:nb], G[:, 1 - par, 0, 0:nb], ACT.Tanh, scale=0.5).then_inc(S["tanhc"], 1)

            def enc_body(c, ahead, extra=None):
                for u in range(CH_T):
                    step(c * CH_T + u, u % 2, 2 * B)
                    if extra is not None:
                        extra(u)
                    if u in (0, 2):
                        seeds_high(c, 1, u // 2)
                    elif ahead and u in (9, 12):
                        seeds_high(c + 1, 0, (u - 9) // 3)

            for d in range(2):
                seeds_high(0, 0, d)
            enc_body(0, True, last_chunk)
            with act.Fori(1, CHUNKS - 1) as c:
                enc_body(c, True)
            enc_body(CHUNKS - 1, False)

            def mlp(u, k):
                if u == 1:
                    act.wait_ge(S["fcen"], k + 1)
                    act.activation(sq[:, :], p_small[0:D, 0:CC], ACT.Square).then_inc(S["fsq"], 1)
                    act.copy(cen[:, :], p_small[0:D, 0:CC]).then_inc(S["cenc"], 1)
                elif u == 7:
                    act.wait_ge(S["u_mm"], 2 * k + 2)
                    act.activation(usq[:, :], p_b[:, 0:256], ACT.Square).then_inc(S["usq"], 1)
                elif u == 8:
                    act.wait_ge(S["r_mm"], k + 1)
                    act.copy(wrow[:, bass.ds(k * CC, CC)], p_a[:, 256:256 + CC]).then_inc(S["wrow"], 1)
                elif u == 9:
                    act.wait_ge(S["uin2"], k + 1)
                    act.activation(uth[:, :], uin2[:, :], ACT.Tanh, scale=GELU_S).then_inc(S["uth"], 1)
                elif u == 12:
                    act.wait_ge(S["ab_mm"], k + 1)
                    act.copy(ab[:, bass.ds(k * 128, 128)], p_x0[:, 0:CC]).then_inc(S["ab"], 1)

            def dec_body(k, behind):
                for u in range(CH_T):
                    step(k * CH_T + (T + u), u % 2, B)
                    if behind:
                        mlp(u, k - 1)

            dec_body(0, False)
            with act.Fori(1, CHUNKS) as k:
                dec_body(k, True)
            for u in range(CH_T):
                mlp(u, CHUNKS - 1)
            store(act, 1)
            store(act, 3)

        @block.vector
        def _(v):
            def seeds_low(c, h, d):
                v.wait_ge(S["seed_a"], 4 * c + (2 * h + d + 1))
                v.tensor_tensor(seed_half(1, h, d), proj_half(h, d), seed_half(0, h, d), ALU.subtract).then_inc(S["seed_b"], 1)

            hm_b = A("headmask").rearrange("p (o m) -> p o m", o=1).broadcast_to([128, 32, 16])

            def group_sums(m, s, loads):
                v.wait_ge(s_x[s], 16 * loads)
                for p in range(PAIRS):
                    last = v.tensor_reduce(qsum[:, bass.ds(m * 32 + p * GS, GS)],
                                           Xv[s][:, p, :, :].rearrange("q w (g c) -> q g w c", c=GS), AX.XY, ALU.add)
                last.then_inc(S["qsum"], 1)

            def pixels(m, s, r):
                v.wait_ge(S["xt_mm"], 4 * m + (XT_ORDER.index(r) + 1))
                v.tensor_copy(xT[:, s, r * 512:r * 512 + 512], xt_bank[r][:, :]).then_inc(xt_copied[1], 1)

            def query(m):
                v.wait_ge(S["qp_mm"], m + 1)
                v.tensor_scalar(qp[:, :], p_small[:, 0:32], A("bq"), float(D // NH) ** -0.5, ALU.add,
                                ALU.mult).then_inc(S["qp"], 1)
                v.wait_ge(S["qp"], m + 1)
                v.tensor_tensor(qm[:, :].rearrange("p (n m) -> p n m", m=16),
                                qp[:, :].rearrange("p (n o) -> p n o", o=1).broadcast_to([128, 32, 16]), hm_b,
                                ALU.mult).then_inc(S["qm"], 1)

            def maxima(m):
                v.wait_ge(S["score_mm"], m + 1)
                v.tensor_tensor(score[:, :], p_b[:, :], A("groupmask"), ALU.add).then_inc(S["score"], 1)
                v.wait_ge(S["score"], m + 1)
                v.tensor_reduce(negmax[:, :], score[:, :].rearrange("p (j m) -> p j m", j=4), AX.X, ALU.max,
                                negate=True).then_inc(S["negmax"], 1)

            def recips(m):
                v.wait_ge(S["exp"], m + 1)
                v.reciprocal(rsum[:, :], esum[:, :]).then_inc(S["rsum"], 1)

            def context_own(n):
                v.wait_ge(S["c_mm"], n + 1)
                v.tensor_tensor(cmask[:, :].rearrange("p (n m) -> p n m", m=16),
                                zB[:, :].rearrange("p (n m) -> p n m", m=16), hm_b, ALU.mult).then_inc(S["cmask"], 1)

            def context(n):
                v.wait_ge(S["cmask"], n + 1)
                v.tensor_reduce(ctxv[:, :], cmask[:, :].rearrange("p (n m) -> p n m", m=16), AX.X,
                                ALU.add).then_inc(S["ctxv"], 1)
                v.wait_ge(S["ctxv"], n + 1)
                v.tensor_scalar(ctxb[:, :], ctxv[:, :], A("bv"), None, ALU.add).then_inc(S["ctxb"], 1)

            def tokens(n, o=zB):
                v.wait_ge(S["o_mm"], n + 1)
                v.tensor_scalar(h1T[:, bass.ds(n * SC, SC)].rearrange("d (g p e) -> d e p g", p=PAIRS, e=2),
                                o[0:D, 0:64].rearrange("d (e p g) -> d e p g", e=2, p=PAIRS),
                                Bc("bo"), None, ALU.add).then_inc(S["h1"], 1)

            def strips(n, u, loads, last, beside=None):
                if not last:
                    group_sums(n + 2, u, loads)
                maxima(n + 1)
                if not last:
                    query(n + 2)
                context_own(n)
                context(n)
                if not last:
                    pixels(n + 2, u, 3)
                recips(n + 1)
                if beside is not None:
                    beside()
                tokens(n)

            v.wait_ge(s_ca, 16)
            v.tensor_scalar(A("wq"), A("wq"), 1.0 / (GS * GS), None, ALU.mult).then_inc(S["wq"], 1)
            group_sums(0, 0, 1)
            pixels(0, 0, 3)
            query(0)
            group_sums(1, 1, 1)
            maxima(0)
            query(1)
            recips(0)
            pixels(1, 1, 3)
            v.wait_ge(s_cb, 16)
            with v.Fori(0, STRIPS // 2 - 1) as i:
                for u in range(2):
                    strips(2 * i + u, u, i + 2, False)
            def text_variances():
                v.wait_ge(S["tsq"], 1)
                v.tensor_reduce(tvar[:, :], txt_sq[:, :, :], AX.X, ALU.add).then_inc(S["tvar"], 1)
                v.wait_ge(S["tvar"], 1)
                v.tensor_scalar(tvar[:, :], tvar[:, :], 1.0 / D, EPS, ALU.mult, ALU.add).then_inc(S["tvar"], 1)
                v.wait_ge(S["tvar"], 2)
                v.tensor_scalar(tr2[:, :].bitcast(I32), tvar[:, :].bitcast(I32), 1, None,
                                ALU.logical_shift_right).then_inc(S["tvar"], 1)
                v.tensor_scalar(tv_nh[:, :], tvar[:, :], -0.5, None, ALU.mult)
                v.wait_ge(S["tvar"], 3)
                v.tensor_scalar(troot[:, :].bitcast(I32), tr2[:, :].bitcast(I32), -1.0, ROOT_MAGIC, ALU.mult,
                                ALU.add).then_inc(S["tseed"], 1)

            v.wait_ge(S["txt"], 3)
            v.tensor_reduce(tmean[:, :], txt[:, :, :], AX.X, ALU.add).then_inc(S["tsum"], 1)
            strips(STRIPS - 2, 0, 0, True, text_variances)
            v.wait_ge(S["tt_mm"], 1)
            v.tensor_copy(tcols[:, 0:4, :], p_x0[0:D, :].rearrange("d (b t) -> d b t", b=4)).then_inc(S["tt_copy"], 1)
            rd = [0]

            def r_(ins):
                rd[0] += 1
                ins.then_inc(S["root"], 1)

            def root():
                v.wait_ge(S["root"], rd[0])

            def root_guess(q, c0, c1):
                c = slice(c0, c1)
                v.wait_ge(S["var"], q)
                r_(v.tensor_scalar(vcol[:, c], p_small[:, c], EPS, None, ALU.add))
                r_(v.tensor_scalar(vhalf[:, c], p_small[:, c], EPS, -0.5, ALU.add, ALU.mult))
                root()
                r_(v.tensor_scalar(rtmp[:, c].bitcast(I32), vcol[:, c].bitcast(I32), 1, None, ALU.logical_shift_right))
                root()
                r_(v.tensor_scalar(rcol[:, c].bitcast(I32), rtmp[:, c].bitcast(I32), -1.0, ROOT_MAGIC, ALU.mult, ALU.add))
                root()

            def root_better(c0, c1):
                c = slice(c0, c1)
                r_(v.tensor_tensor(rtmp[:, c], rcol[:, c], rcol[:, c], ALU.mult))
                root()
                r_(v.tensor_tensor(rtmp[:, c], rtmp[:, c], vhalf[:, c], ALU.mult))
                root()
                r_(v.scalar_tensor_tensor(rcol[:, c], rtmp[:, c], 1.5, rcol[:, c], ALU.add, ALU.mult))
                root()

            def normalised(q, c0, c1):
                c = slice(c0 * CC, c1 * CC)
                v.wait_ge(S["spread"], q)
                v.tensor_tensor(xnT[0:D, c], p_b[0:D, c], spread[:, c], ALU.mult).then_inc(S["xnT"], 1)

            root_guess(1, 0, EARLY)
            for _ in range(3):
                root_better(0, EARLY)
            assert rd[0] == ROOTS
            context_own(STRIPS - 1)
            v.wait_ge(S["tn_mm"], 1)
            v.tensor_copy(tncols[:, 0:4, :], p_x0[0:D, :].rearrange("d (b t) -> d b t", b=4)).then_inc(S["tn_copy"], 1)
            normalised(1, 0, EARLY)
            context(STRIPS - 1)

            def last_chunk(u):
                if u == 1:
                    tokens(STRIPS - 1, p_small)
                elif u == 5:
                    root_guess(2, EARLY, IMG_CHUNKS)
                elif u in (6, 7, 8):
                    root_better(EARLY, IMG_CHUNKS)
                elif u == 14:
                    normalised(2, EARLY, IMG_CHUNKS)

            def step(t, par, nb, h_out):
                v.wait_ge(S["gates"], t + 2)
                v.scalar_tensor_tensor(prod[:, :, 0:nb], G[:, par, 2:4, 0:nb], 1.0, G[:, par, 0:2, 0:nb], ALU.add,
                                       ALU.mult).then_inc(S["prod"], 1)
                v.wait_ge(S["prod"], t + 1)
                v.scalar_tensor_tensor(G[:, 1 - par, 0, 0:nb], prod[:, 0, 0:nb], 0.5, prod[:, 1, 0:nb], ALU.mult,
                                       ALU.add).then_inc(S["cell"], 1)
                v.wait_ge(S["ogate"], t + 2)
                v.tensor_scalar(osc[:, 0:nb], G[:, par, 4, 0:nb], 1.0, 0.5 * H_SCALE, ALU.add,
                                ALU.mult).then_inc(S["osc"], 1)
                v.wait_ge(S["tanhc"], t + 1)
                v.wait_ge(S["osc"], t + 1)
                v.tensor_tensor(ha[:, 0:nb], osc[:, 0:nb], tc[:, 0:nb], ALU.mult).then_inc(S["ha"], 1)
                v.tensor_tensor(h_out, osc[:, 0:nb], tc[:, 0:nb], ALU.mult).then_inc(S["hfull"], 1)
                v.wait_ge(S["hfull"], t + 1)
                v.tensor_tensor(hb[:, 0:nb], h_out, ha[:, 0:nb], ALU.subtract).then_inc(S["hb"], 1)

            def enc_body(c, ahead, extra=None):
                for u in range(CH_T):
                    step(c * CH_T + u, u % 2, 2 * B, H[:, :])
                    if extra is not None:
                        extra(u)
                    if u in (1, 3):
                        seeds_low(c, 1, u // 2)
                    elif ahead and u in (10, 13):
                        seeds_low(c + 1, 0, (u - 10) // 3)

            v.wait_ge(S["memset"], 5)
            for d in range(2):
                seeds_low(0, 0, d)
            enc_body(0, True, last_chunk)
            with v.Fori(1, CHUNKS - 1) as c:
                enc_body(c, True)
            enc_body(CHUNKS - 1, False)
            v.wait_ge(S["lat"], 1)
            v.scalar_tensor_tensor(zc[:, :].rearrange("p (g b) -> p g b", g=4), p_t[:, 0:32].rearrange("p (g b) -> p g b", g=4),
                                   SEED_SCALE / (H_SCALE * U_SCALE),
                                   A("bd").rearrange("p (g o) -> p g o", o=1).broadcast_to([128, 4, B]), ALU.mult,
                                   ALU.add).then_inc(S["zc"], 1)
            v.memset(G[:, 0, 0, :], 0.0).then_inc(S["zc"], 1)
            v.memset(ha[:, :], 0.0).then_inc(S["zc"], 1)
            v.memset(hb[:, :], 0.0).then_inc(S["zc"], 1)
            v.wait_ge(S["zc"], 4)
            v.tensor_copy(zcs[0][:, :], zc[:, :]).then_inc(S["zcs"], 1)
            v.wait_ge(S["zcs"], 1)
            v.tensor_tensor(zcs[1][:, :], zc[:, :], zcs[0][:, :], ALU.subtract).then_inc(S["zcs"], 1)

            def mlp(u, k):
                if u == 0:
                    v.wait_ge(S["f_mm"], k + 1)
                    v.scalar_tensor_tensor(h2[:, :], p_t[0:D, 0:CC], Bc("boA"), h1T[:, bass.ds(k * CC, CC)], ALU.add,
                                           ALU.add).then_inc(S["h2"], 1)
                elif u == 2:
                    v.wait_ge(S["fvar"], k + 1)
                    v.tensor_scalar(var[:, :], p_a[:, 0:1], EPS, None, ALU.add).then_inc(S["varp"], 1)
                    v.tensor_scalar(var_nh[:, :], p_a[:, 0:1], EPS, -0.5, ALU.add, ALU.mult)
                    v.wait_ge(S["varp"], 2 * k + 1)
                    v.tensor_scalar(ru[:, :].bitcast(I32), var[:, :].bitcast(I32), 1, None,
                                    ALU.logical_shift_right).then_inc(S["varp"], 1)
                    v.wait_ge(S["varp"], 2 * k + 2)
                    v.tensor_scalar(rstd[:, :].bitcast(I32), ru[:, :].bitcast(I32), -1.0, ROOT_MAGIC, ALU.mult,
                                    ALU.add).then_inc(S["vseed"], 1)
                elif u == 5:
                    v.wait_ge(S["fbc"], k + 1)
                    v.wait_ge(S["cenc"], k + 1)
                    v.tensor_tensor(xn[0:D, :], p_a[0:D, CC:2 * CC], cen[:, :], ALU.mult).then_inc(S["xn"], 1)
                elif u == 6:
                    v.wait_ge(S["xn"], k + 1)
                    v.tensor_tensor(parts[0:D, :], h2[:, :], xn[0:D, :], ALU.add).then_inc(S["at"], 1)
                elif u == 7:
                    v.wait_ge(S["usq"], k + 1)
                    v.tensor_scalar(uin[:, :], usq[:, :], GELU_C, 1.0, ALU.mult, ALU.add).then_inc(S["uin"], 1)
                elif u == 8:
                    v.wait_ge(S["uin"], k + 1)
                    v.tensor_tensor(uin2[:, :], uin[:, :], p_b[:, 0:256], ALU.mult).then_inc(S["uin2"], 1)
                elif u == 9:
                    v.wait_ge(S["uth"], k + 1)
                    v.scalar_tensor_tensor(ug[:, :], uth[:, :], 1.0, p_b[:, 0:256], ALU.add, ALU.mult).then_inc(S["ug"], 1)
                elif u == 11:
                    v.wait_ge(S["y2_mm"], k + 1)
                    v.wait_ge(S["wrow"], k + 1)
                    v.scalar_tensor_tensor(parts[D:128, :], p_x1[D:128, 0:CC], A("b2")[D:128, :],
                                           wrow[D:128, bass.ds(k * CC, CC)], ALU.add, ALU.mult).then_inc(S["bt"], 1)

            def dec_body(k, behind, extra=None):
                for u in range(CH_T):
                    step(k * CH_T + (T + u), u % 2, B, H[:, 0:B] if u == 0 else hist[:, u * B:u * B + B])
                    if behind:
                        mlp(u, k - 1)
                    if u == 1:
                        v.tensor_copy(hist[:, 0:B], H[:, 0:B])
                    if extra is not None:
                        extra(u)

            def rival_columns(hf):
                v.wait_ge(S["wc_mm"], hf + 1)
                v.tensor_copy(wcol[:, 8 * hf:8 * hf + 8], p_t[0:HALF, 256 + 8 * hf:256 + 8 * hf + 8]).then_inc(S["wcol"], 1)

            def compare(dst, i, j, op, lo=0, hi=HALF):
                return v.tensor_tensor(tb(dst)[:, lo:hi, :], own(i)[:, lo:hi, :],
                                       rival(j, hi - lo), op)

            def ties(j, lo=0, hi=HALF):
                return v.tensor_tensor(tb(tie[j])[:, lo:hi, :], tb(equal[j])[:, lo:hi, :], earlier(lo, hi), ALU.mult)

            def first_half_ranks(u):
                mid = HALF // 2
                if u == 4:
                    rival_columns(0)
                elif u == 5:
                    v.wait_ge(S["wcol"], 1)
                    compare(equal[0], 0, 0, ALU.is_equal, 0, mid).then_inc(S["equal"], 1)
                elif u == 10:
                    compare(equal[0], 0, 0, ALU.is_equal, mid, HALF).then_inc(S["equal"], 1)
                elif u in (12, 13):
                    h = u - 12
                    compare(beats[0][0], 0, 0, ALU.is_lt, mid * h, mid * (h + 1)).then_inc(S["beats"], 1)
                elif u in (14, 15):
                    h = u - 14
                    v.wait_ge(S["equal"], 2)
                    ties(0, mid * h, mid * (h + 1)).then_inc(S["beats"], 1)

            dec_body(0, False)
            with v.Fori(1, CHUNKS - 1) as k:
                dec_body(k, True)
            dec_body(CHUNKS - 1, True, first_half_ranks)
            for u in range(CH_T):
                mlp(u, CHUNKS - 1)
                if u == 9:
                    rival_columns(1)
                    v.wait_ge(S["wcol"], 2)
                    compare(equal[1], 1, 1, ALU.is_equal).then_inc(S["equal"], 1)
            compare(beats[0][1], 1, 0, ALU.is_le).then_inc(S["beats"], 1)
            compare(beats[1][1], 1, 1, ALU.is_lt).then_inc(S["beats"], 1)
            compare(beats[1][0], 0, 1, ALU.is_lt).then_inc(S["beats"], 1)
            v.wait_ge(S["rank"], 1)
            v.tensor_scalar(keep[:, :], p_small[:, 0:CHUNKS], KEEP - 0.5, None, ALU.is_lt).then_inc(S["keep"], 1)
            v.wait_ge(S["keep"], 1)
            abv = ab[:, :].rearrange("p (k s d) -> p k s d", k=CHUNKS, s=2)
            for k in range(CHUNKS):
                v.scalar_tensor_tensor(fin[:, k, :], abv[:, k, 1, :], keep[:, k:k + 1], abv[:, k, 0, :], ALU.mult,
                                       ALU.add).then_inc(S["fin"], 1)


def kernel(**inputs):
    import numpy as np
    import concourse.bacc as bacc
    from concourse.bass_utils import run_bass_kernel_spmd

    f = np.float32
    inp = {k: np.asarray(v) for k, v in inputs.items()}
    pa, pb = np.zeros((128, PA_N), f), np.zeros((65, PB_N), f)

    def put(name, val):
        val = np.asarray(val, f)
        pa[:val.shape[0], PA[name][0]:PA[name][1]] = val

    def putb(name, val):
        val = np.asarray(val, f)
        pb[:val.shape[0], PB[name][0]:PB[name][1]] = val

    def diagonal(m):
        z = np.zeros((128, 128), f)
        z[:64, :64] = m
        z[64:, 64:] = m
        return z

    def gates(m):
        m = m.reshape(m.shape[0], 4, HID)
        return np.concatenate([m[:, k] for k in (2, 1, 0, 3)], axis=1)

    def twice(v):
        return np.concatenate([v, v])[:, None]

    eye = np.eye(128, dtype=f)
    put("ident", eye)
    put("wq", diagonal(inp["L0_tok_Wq"].T))
    put("wk", diagonal(inp["L0_tok_Wk"]))
    put("wv", diagonal(inp["L0_tok_Wv"].T))
    for e in range(2):
        wo, res = np.zeros((128, D), f), np.zeros((128, D), f)
        wo[64 * e:64 * e + 64] = inp["L0_tok_Wo"].T
        res[64 * e:64 * e + 64] = np.eye(D, dtype=f) / (GS * GS)
        put(f"wo{e}", wo)
        put(f"res{e}", res)
    q, c = np.arange(128)[:, None], np.arange(16)[None]
    put("headmask", (q // 64 == c // 8) & (q % 64 // 8 == c % 8))
    row, pix = np.arange(128)[:, None], np.arange(512)[None]
    put("groupmask", np.where(row // 16 % 2 == pix % 16 // 8, 0.0, NEG))
    put("bq", twice(inp["L0_tok_bq"]))
    put("bv", twice(inp["L0_tok_bv"]))
    for n in "fbd":
        put("U" + n, gates(inp["L0_attn_U" + n]))
    wd = gates(inp["L0_attn_Wd"])
    put("Wd0", wd[:HID])
    put("Wd1", wd[HID:])
    put("bd", gates(inp["L0_attn_bd"][None]).reshape(4, HID).T)
    put("Wo", inp["L0_attn_Wo"])
    put("w2a", np.pad(inp["L0_ffn_w2"][:128], ((0, 0), (D, 0))))
    put("w2b", np.pad(inp["L0_ffn_w2"][128:], ((0, 0), (D, 0))))
    put("before", np.arange(HALF)[:, None] < np.arange(HALF)[None])
    putb("center", np.tile(np.eye(D) - 1.0 / D, 2))
    putb("mean", np.full((D, 128), 1.0 / D))
    putb("bo", inp["L0_tok_bo"][:, None])
    putb("boA", inp["L0_attn_bo"][:, None])
    put("b2", twice(inp["L0_ffn_b2"]))
    for n, b in (("Wf", "bf"), ("Wb", "bb")):
        putb(n, gates(np.concatenate([inp["L0_attn_" + n], inp["L0_attn_" + b][None]])))
    putb("w1", np.concatenate([inp["L0_ffn_w1"], inp["L0_ffn_b1"][None]]))
    putb("wr", np.repeat(np.concatenate([inp["L0_ffn_wr"], inp["L0_ffn_br"][None]]), 128, axis=1))

    arrays = {
        "x": np.ascontiguousarray(inp["x"]),
        "ids": np.ascontiguousarray(inp["x_txt"].T),
        "table": np.ascontiguousarray(inp["L0_txt_shared_embedding"]),
        "hashw": np.ascontiguousarray(inp["L0_txt_hash_weights_table"]),
        "packa": pa, "packb": pb,
    }
    nc = bacc.Bacc("TRN2", target_bir_lowering=False, num_devices=1)
    aps = [nc.dram_tensor(n, a.shape, mybir.dt.from_np(a.dtype), kind="ExternalInput").ap() for n, a in arrays.items()]
    out = nc.dram_tensor("out", (TOK, D), F32, kind="ExternalOutput").ap()
    build(nc, *aps, out)
    r = run_bass_kernel_spmd(nc, [arrays], core_ids=[0])
    got = r.results[0]["out"].reshape(T, B, D)
    return np.ascontiguousarray(got.transpose(1, 0, 2))
```
